# Optimizing a Trainium2 kernel written in Bass

```python
import numpy as np
import jax
import jax.numpy as jnp

def _softmax(x, axis=-1):
    return jax.nn.softmax(x, axis=axis)

def _gelu(x):
    return jax.nn.gelu(x, approximate=True)

def _silu(x):
    return jax.nn.silu(x)

def _sigmoid(x):
    return jax.nn.sigmoid(x)

def _layernorm(x, axis=-1, eps=1e-05):
    m = jnp.mean(x, axis=axis, keepdims=True)
    v = jnp.var(x, axis=axis, keepdims=True)
    return (x - m) / jnp.sqrt(v + eps)

def _scatter_add(tgt, idx, src, axis=0):
    return tgt.at[idx].add(src)

def _segment_sum(src, seg, n):
    return jax.ops.segment_sum(src, seg, n)
kernel_name = 'mk_hybrid_d1_jaxref_r8_1af56e'

def setup_inputs(seed: int=0):
    np.random.seed(seed)
    _w = jnp.asarray

    def _L0_attn_a_setup():
        import jax, jax.numpy as jnp
        import numpy as np
        N_EMBD = 128
        N_ATTN = 128
        N_HEAD = 16
        N_LAYER = 12
        LAYER_ID = 5
        CTX = 256
        BATCH = 8
        HEAD_SIZE = N_ATTN // N_HEAD
        K_CLAMP = 60.0
        K_EPS = 1e-16

        def _time_decay_init():
            first = 1
            f1 = 3.0 + (LAYER_ID - first) / (N_LAYER - 1 - first) * (1.2 - 3.0)
            f2 = 0.65 + (LAYER_ID - first) / (N_LAYER - 1 - first) * (0.4 - 0.65)
            if LAYER_ID == first:
                f1 += 0.5
            if LAYER_ID == N_LAYER - 2:
                f2 = 0.4
            if LAYER_ID == N_LAYER - 1:
                f2 = 0.37
            h = np.arange(N_HEAD, dtype=np.float64)
            decay_speed = np.power(f2, h / (N_HEAD - 1) * 7) * f1
            return np.log(decay_speed).astype(np.float32)[:, None]
        key = jax.random.key(seed)
        ks = jax.random.split(key, 5)
        x = jax.random.normal(ks[0], (BATCH, CTX, N_EMBD), dtype=jnp.float32)
        tm = np.ones((1, 1, N_EMBD), dtype=np.float32)
        tm[0, 0, :N_EMBD // 2] = 0.0
        scale = 0.02
        return {'x': x, 'time_decay': jnp.asarray(_time_decay_init()), 'time_first': jnp.full((N_HEAD, 1), np.log(0.3), dtype=jnp.float32), 'time_mix': jnp.asarray(tm), 'Wk': jax.random.normal(ks[1], (N_ATTN, N_EMBD), dtype=jnp.float32) * scale, 'Wv': jax.random.normal(ks[2], (N_ATTN, N_EMBD), dtype=jnp.float32) * scale, 'Wr': jax.random.normal(ks[3], (N_ATTN, N_EMBD), dtype=jnp.float32) * scale, 'Wo': jax.random.normal(ks[4], (N_EMBD, N_ATTN), dtype=jnp.float32) * scale}
    _L0_attn_a_in = _L0_attn_a_setup()

    def _L0_attn_b_setup():
        import jax, jax.numpy as jnp
        import numpy as np
        DIM = 128
        DIM_HEADS = 128
        HEADS = 8
        DHEAD = DIM_HEADS // HEADS
        EPS = 1e-06

        def _l2norm(t, axis=-1):
            n = jnp.sqrt(jnp.sum(t * t, axis=axis, keepdims=True))
            return t / jnp.maximum(n, 1e-12)
        key = jax.random.key(seed)
        k1, k2, k3 = jax.random.split(key, 3)
        x = jax.random.normal(k1, (8, 512, DIM), dtype=jnp.float32)
        norm_weight = jnp.ones((DIM,), dtype=jnp.float32)
        w_qkv = jax.random.normal(k2, (3 * DIM_HEADS, DIM), dtype=jnp.float32) * (1.0 / np.sqrt(DIM))
        temperature = jnp.zeros((HEADS, 1, 1), dtype=jnp.float32)
        w_out = jax.random.normal(k3, (DIM, DIM_HEADS), dtype=jnp.float32) * (1.0 / np.sqrt(DIM_HEADS))
        return {'x': x, 'norm_weight': norm_weight, 'w_qkv': w_qkv, 'temperature': temperature, 'w_out': w_out}
    _L0_attn_b_in = _L0_attn_b_setup()

    def _L0_ffn_setup():
        import jax, jax.numpy as jnp
        import numpy as np
        E = 8
        K = 2
        D = 128
        H = 342
        B, S = (2, 256)

        def _moe_forward(x, centroid, Wg, bg, W1, b1, W2, b2):
            T = x.shape[0] * x.shape[1]
            xs = x.reshape(T, D)
            d2 = jnp.sum(xs * xs, axis=-1, keepdims=True) + jnp.sum(centroid * centroid, axis=-1)[None, :] - 2.0 * (xs @ centroid.T)
            dist = jnp.sqrt(jnp.maximum(d2, 1e-12))
            w, sel = jax.lax.top_k(dist, K)
            w = jax.nn.softmax(w.astype(jnp.float32), axis=1).astype(x.dtype)
            we = jnp.zeros((T, E), dtype=x.dtype).at[jnp.arange(T)[:, None], sel].add(w)
            out = jnp.zeros_like(xs)
            for e in range(E):
                h = jax.nn.silu(xs @ Wg[e] + bg[e]) * (xs @ W1[e] + b1[e])
                out = out + we[:, e:e + 1] * (h @ W2[e] + b2[e])
            return out.reshape(x.shape)
        key = jax.random.key(seed)
        ks = jax.random.split(key, 9)
        scale = 0.02
        return {'x': jax.random.normal(ks[0], (B, S, D), dtype=jnp.float32), 'centroid': jax.random.normal(ks[1], (E, D), dtype=jnp.float32), 'Wg': jax.random.normal(ks[2], (E, D, H), dtype=jnp.float32) * scale, 'bg': jnp.zeros((E, H), dtype=jnp.float32), 'W1': jax.random.normal(ks[3], (E, D, H), dtype=jnp.float32) * scale, 'b1': jnp.zeros((E, H), dtype=jnp.float32), 'W2': jax.random.normal(ks[4], (E, H, D), dtype=jnp.float32) * scale, 'b2': jnp.zeros((E, D), dtype=jnp.float32)}
    _L0_ffn_in = _L0_ffn_setup()
    _d = {'L0_attn_a_x': _L0_attn_a_in['x'], 'L0_attn_a_time_decay': _L0_attn_a_in['time_decay'], 'L0_attn_a_time_first': _L0_attn_a_in['time_first'], 'L0_attn_a_time_mix': _L0_attn_a_in['time_mix'], 'L0_attn_a_Wk': _L0_attn_a_in['Wk'], 'L0_attn_a_Wv': _L0_attn_a_in['Wv'], 'L0_attn_a_Wr': _L0_attn_a_in['Wr'], 'L0_attn_a_Wo': _L0_attn_a_in['Wo'], 'L0_attn_b_norm_weight': _L0_attn_b_in['norm_weight'], 'L0_attn_b_w_qkv': _L0_attn_b_in['w_qkv'], 'L0_attn_b_temperature': _L0_attn_b_in['temperature'], 'L0_attn_b_w_out': _L0_attn_b_in['w_out'], 'L0_ffn_centroid': _L0_ffn_in['centroid'], 'L0_ffn_Wg': _L0_ffn_in['Wg'], 'L0_ffn_bg': _L0_ffn_in['bg'], 'L0_ffn_W1': _L0_ffn_in['W1'], 'L0_ffn_b1': _L0_ffn_in['b1'], 'L0_ffn_W2': _L0_ffn_in['W2'], 'L0_ffn_b2': _L0_ffn_in['b2']}
    _x0 = _d['L0_attn_a_x']
    _d['L0_attn_a_x'] = jax.random.normal(jax.random.fold_in(jax.random.key(seed), 1), (16, 256, 128), dtype=_x0.dtype)
    del _x0
    return _d

def reference(L0_attn_a_x, L0_attn_a_time_decay, L0_attn_a_time_first, L0_attn_a_time_mix, L0_attn_a_Wk, L0_attn_a_Wv, L0_attn_a_Wr, L0_attn_a_Wo, L0_attn_b_norm_weight, L0_attn_b_w_qkv, L0_attn_b_temperature, L0_attn_b_w_out, L0_ffn_centroid, L0_ffn_Wg, L0_ffn_bg, L0_ffn_W1, L0_ffn_b1, L0_ffn_W2, L0_ffn_b2):

    def _L0_attn_a_ref(x, time_decay, time_first, time_mix, Wk, Wv, Wr, Wo):
        import jax, jax.numpy as jnp
        import numpy as np
        N_EMBD = 128
        N_ATTN = 128
        N_HEAD = 16
        N_LAYER = 12
        LAYER_ID = 5
        CTX = 256
        BATCH = 8
        HEAD_SIZE = N_ATTN // N_HEAD
        K_CLAMP = 60.0
        K_EPS = 1e-16

        def _time_decay_init():
            first = 1
            f1 = 3.0 + (LAYER_ID - first) / (N_LAYER - 1 - first) * (1.2 - 3.0)
            f2 = 0.65 + (LAYER_ID - first) / (N_LAYER - 1 - first) * (0.4 - 0.65)
            if LAYER_ID == first:
                f1 += 0.5
            if LAYER_ID == N_LAYER - 2:
                f2 = 0.4
            if LAYER_ID == N_LAYER - 1:
                f2 = 0.37
            h = np.arange(N_HEAD, dtype=np.float64)
            decay_speed = np.power(f2, h / (N_HEAD - 1) * 7) * f1
            return np.log(decay_speed).astype(np.float32)[:, None]
        B, T, C = x.shape
        H = time_decay.shape[0]
        D = Wk.shape[0] // H
        xs = jnp.pad(x, ((0, 0), (1, 0), (0, 0)))[:, :T]
        xm = x * time_mix + xs * (1.0 - time_mix)
        k = jnp.exp(jnp.minimum(xm @ Wk.T, K_CLAMP))
        v = xm @ Wv.T
        r = xm @ Wr.T
        kv = k * v
        lag = jnp.arange(T)[:, None] - jnp.arange(T)[None, :]
        dec = jnp.exp(time_decay[:, 0])[:, None, None]
        e = jnp.exp(-dec * jnp.maximum(lag - 1, 0).astype(jnp.float32))
        Wm = jnp.where(lag >= 1, e, 0.0)
        Wm = jnp.where(lag == 0, jnp.exp(time_first[:, 0])[:, None, None], Wm)
        kh = k.reshape(B, T, H, D)
        kvh = kv.reshape(B, T, H, D)
        wkv = jnp.einsum('htu,buhd->bthd', Wm, kvh).reshape(B, T, H * D)
        sum_k = jnp.einsum('htu,buhd->bthd', Wm, kh).reshape(B, T, H * D) + K_EPS
        rwkv = jax.nn.sigmoid(r) * wkv / sum_k
        return rwkv @ Wo.T

    def _L0_attn_b_ref(x, norm_weight, w_qkv, temperature, w_out):
        import jax, jax.numpy as jnp
        import numpy as np
        DIM = 128
        DIM_HEADS = 128
        HEADS = 8
        DHEAD = DIM_HEADS // HEADS
        EPS = 1e-06

        def _l2norm(t, axis=-1):
            n = jnp.sqrt(jnp.sum(t * t, axis=axis, keepdims=True))
            return t / jnp.maximum(n, 1e-12)
        b, n, _ = x.shape
        ms = jnp.mean(x * x, axis=-1, keepdims=True)
        xn = x * jax.lax.rsqrt(ms + EPS) * norm_weight
        qkv = jnp.einsum('bnc,oc->bno', xn, w_qkv)
        qkv = qkv.reshape(b, n, 3, HEADS, DHEAD).transpose(2, 0, 3, 4, 1)
        q, k, v = (qkv[0], qkv[1], qkv[2])
        q = _l2norm(q)
        k = _l2norm(k)
        q = q * jnp.exp(temperature)
        sim = jnp.einsum('bhin,bhjn->bhij', q, k)
        attn = jax.nn.softmax(sim, axis=-1)
        out = jnp.einsum('bhij,bhjn->bhin', attn, v)
        out = out.transpose(0, 3, 1, 2).reshape(b, n, HEADS * DHEAD)
        return jnp.einsum('bnc,oc->bno', out, w_out)

    def _L0_ffn_ref(x, centroid, Wg, bg, W1, b1, W2, b2):
        import jax, jax.numpy as jnp
        import numpy as np
        E = 8
        K = 2
        D = 128
        H = 342
        B, S = (2, 256)

        def _moe_forward(x, centroid, Wg, bg, W1, b1, W2, b2):
            T = x.shape[0] * x.shape[1]
            xs = x.reshape(T, D)
            d2 = jnp.sum(xs * xs, axis=-1, keepdims=True) + jnp.sum(centroid * centroid, axis=-1)[None, :] - 2.0 * (xs @ centroid.T)
            dist = jnp.sqrt(jnp.maximum(d2, 1e-12))
            w, sel = jax.lax.top_k(dist, K)
            w = jax.nn.softmax(w.astype(jnp.float32), axis=1).astype(x.dtype)
            we = jnp.zeros((T, E), dtype=x.dtype).at[jnp.arange(T)[:, None], sel].add(w)
            out = jnp.zeros_like(xs)
            for e in range(E):
                h = jax.nn.silu(xs @ Wg[e] + bg[e]) * (xs @ W1[e] + b1[e])
                out = out + we[:, e:e + 1] * (h @ W2[e] + b2[e])
            return out.reshape(x.shape)
        return _moe_forward(x, centroid, Wg, bg, W1, b1, W2, b2)
    x = L0_attn_a_x
    x = x + _L0_attn_a_ref(_layernorm(x, axis=-1), L0_attn_a_time_decay, L0_attn_a_time_first, L0_attn_a_time_mix, L0_attn_a_Wk, L0_attn_a_Wv, L0_attn_a_Wr, L0_attn_a_Wo)
    x = x + _L0_ffn_ref(_layernorm(x, axis=-1), L0_ffn_centroid, L0_ffn_Wg, L0_ffn_bg, L0_ffn_W1, L0_ffn_b1, L0_ffn_W2, L0_ffn_b2)
    x = x + _L0_attn_b_ref(_layernorm(x, axis=-1), L0_attn_b_norm_weight, L0_attn_b_w_qkv, L0_attn_b_temperature, L0_attn_b_w_out)
    x = x + _L0_ffn_ref(_layernorm(x, axis=-1), L0_ffn_centroid, L0_ffn_Wg, L0_ffn_bg, L0_ffn_W1, L0_ffn_b1, L0_ffn_W2, L0_ffn_b2)
    return x

_drawn_inputs = setup_inputs


def setup_inputs(seed=0):
    import zlib

    import numpy as np

    out = dict(_drawn_inputs(seed))
    spreads = {'L0_attn_a_time_first': (-1.2039728164672852, 0.6),
     'L0_attn_b_norm_weight': (1.0, 0.588),
     'L0_attn_b_temperature': (0.0, 0.8),
     'L0_ffn_bg': (0.0, 0.8),
     'L0_ffn_b1': (0.0, 0.8),
     'L0_ffn_b2': (0.0, 0.1)}
    factors = {'L0_attn_a_time_decay': 5.635,
     'L0_attn_a_time_mix': 6.924,
     'L0_attn_a_Wk': 8.0,
     'L0_attn_a_Wv': 4.185,
     'L0_attn_a_Wr': 8.0,
     'L0_attn_a_Wo': 4.24,
     'L0_ffn_Wg': 3.768,
     'L0_ffn_W1': 3.78,
     'L0_ffn_W2': 3.42}
    for name, (base, spread) in spreads.items():
        noise = np.random.default_rng([zlib.crc32(name.encode()), seed]).standard_normal(out[name].shape)
        drawn = base * np.exp(spread * noise) if base else spread * noise
        out[name] = jnp.asarray(drawn.astype(out[name].dtype))
    for name, factor in factors.items():
        out[name] = (out[name] * factor).astype(out[name].dtype)
    return out
```

```python
import concourse.bass as bass
from concourse import mybir
from contextlib import ExitStack

P = 128
BATCH, SEQ, DIM = 16, 256, 128
TOKENS = BATCH * SEQ
HALVES = 2
TILES = TOKENS // P
TH = TILES // HALVES
BH = BATCH // HALVES
GROUPS = TH // 4
HEADS_A, DH_A = 16, 8
HEADS_B, DH_B = 8, 16
EXPERTS, HID = 8, 342
CH, NCH = 114, 3
CHOICES = 2
SLOT_TILES = (TH * P * CHOICES + EXPERTS * (P - 1)) // P
ALL_SLOT_TILES = HALVES * SLOT_TILES
SLOTS = ALL_SLOT_TILES * P
UNROLL = 6
assert ALL_SLOT_TILES % UNROLL == 0 and SLOT_TILES % 3 == 0
LN_EPS, RMS_EPS, K_EPS, K_CLAMP, DIST_MIN = 1e-5, 1e-6, 1e-16, 60.0, 1e-12
RSQRT_SEED = float(0x5F3759DF)
A_STEPS, R_STEPS, B_STEPS, F_STEPS = 33, 70, 82, 2


class Chain:

    def __init__(self, eng, sem, start, per_round):
        self.eng, self.sem, self.start, self.per_round, self.n = eng, sem, start, per_round, 0

    def then(self, ins):
        ins.then_inc(self.sem, 1)
        self.n += 1
        return ins

    def wait(self):
        self.eng.wait_ge(self.sem, self.start + self.n)

    def step(self, ins):
        self.then(ins)
        self.wait()

    def close(self):
        assert self.n == self.per_round, (self.sem, self.n, self.per_round)


def build(nc, d, out):
    f32, i32, u32 = mybir.dt.float32, mybir.dt.int32, mybir.dt.uint32
    ACT, ALU, AX = mybir.ActivationFunctionType, mybir.AluOpType, mybir.AxisListType
    nc.disable_value_cache = True
    sorted_x = nc.dram_tensor("sorted_x", [SLOTS, DIM], f32, kind="Internal").ap()
    sorted_y = nc.dram_tensor("sorted_y", [SLOTS, DIM], f32, kind="Internal").ap()
    x_tiles = d["L0_attn_a_x"].rearrange("b (t p) d -> p (b t) d", p=P)
    out_tiles = out.rearrange("b (t p) d -> p (b t) d", p=P)
    with ExitStack() as ctx:
        def sb(name, shape, dt=f32):
            return ctx.enter_context(nc.sbuf_tensor(name, shape, dt))

        def sem(name):
            return ctx.enter_context(nc.semaphore(name))

        X = sb("X", [P, TILES, DIM])
        xn = sb("xn", [P, TH, DIM])
        xn_moe = sb("xn_moe", [P, TH, DIM])
        kv = sb("kv", [P, TH, 2, DIM])
        picked = kv
        gate = sb("gate", [P, TH, DIM])
        rwkv = sb("rwkv", [P, TH, DIM])
        xT_half = rwkv
        decay = sb("decay", [P, HEADS_A, 2 * P])
        wgu = sb("wgu", [P, EXPERTS, 2, HID])
        w2 = sb("w2", [CH, EXPERTS, NCH, DIM])
        bias_gu = sb("bias_gu", [P, EXPERTS, 2, HID])
        bias_2 = sb("bias_2", [P, EXPERTS, DIM])
        ident = sb("ident", [P, P])
        ones = sb("ones", [P, P])
        later = sb("later", [P, P])
        same_head = sb("same_head", [P, HEADS_B, DH_B])
        lag = sb("lag", [P, 2 * P])
        rank = sb("rank", [P, TH, EXPERTS])
        not_first = sb("not_first", [P, EXPERTS, TH])
        slot_no = sb("slot_no", [P, SLOT_TILES, EXPERTS])
        raw = sb("raw", [P, 8, DIM])
        cent = sb("cent", [EXPERTS, DIM])
        wT = sb("wT", [P, 3, DIM])
        woT = sb("woT", [P, DIM])
        wqkT = sb("wqkT", [P, 2, DIM])
        w_outT = sb("w_outT", [P, DIM])
        centT = sb("centT", [P, EXPERTS])
        centT2 = sb("centT2", [P, EXPERTS])
        cent_sq = sb("cent_sq", [P, EXPERTS])
        mixc = sb("mixc", [P, 4])
        rates = sb("rates", [P, 4, HEADS_A])
        mixed = sb("mixed", [P, 2, 4 * P])
        kmin = sb("kmin", [P, 4, DIM])
        den = sb("den", [P, 2, 4, BH, DH_A])
        rec = sb("rec", [P, 2, 4, BH, DH_A])
        yT = sb("yT", [P, 2, 4 * P])
        stats = sb("stats", [P, TH, 6])
        mv = sb("mv", [P, TH, 2])
        scale = sb("scale", [P, TH])
        small = sb("small", [P, 4, P])
        qk = gate[:, 0:8, :].rearrange("p (s t k) c -> p s t (k c)", s=2, t=2)
        qk_sq = gate[:, 8:16, :].rearrange("p (s t k) c -> p s t (k c)", s=2, t=2)
        gram = sb("gram", [P, 2, 2, HEADS_B, DH_B])
        sims = sb("sims", [P, BH, 2, DH_B])
        qnorm = sb("qnorm", [P, BH])
        att = sb("att", [P, BH, DH_B])
        att_diag = sb("att_diag", [P, BH, HEADS_B, DH_B])
        folded = sb("folded", [P, 2, 4, DIM])
        dist = sb("dist", [P, TH, EXPERTS])
        t8 = sb("t8", [P, TH, EXPERTS])
        onehot = sb("onehot", [P, 2, TH, EXPERTS])
        mask = sb("mask", [P, TH, EXPERTS])
        counts = sb("counts", [P, EXPERTS, TH])
        upto = sb("upto", [P, EXPERTS, TH])
        top = sb("top", [P, 2, TH])
        far = sb("far", [P, 2, TH])
        pos_f = sb("pos_f", [P, TH, 2])
        exp_e = sb("exp_e", [P, 4, EXPERTS])
        exp_i = sb("exp_i", [P, EXPERTS], i32)
        carrier = sb("carrier", [P, 1])
        half_base = sb("half_base", [P, HALVES])
        slot_cmp = sb("slot_cmp", [P, SLOT_TILES, EXPERTS])
        slot_f = sb("slot_f", [P, SLOT_TILES])
        slot_of = sb("slot_of", [P, HALVES, TH, 2], i32)
        weight = sb("weight", [P, HALVES, TH, 2])
        expert_of = sb("expert_of", [P, ALL_SLOT_TILES], i32)
        ex_x = sb("ex_x", [P, 3, DIM])
        ex_xT = sb("ex_xT", [P, 2, P])
        ex_g = sb("ex_g", [P, 2, HID])
        ex_s = sb("ex_s", [P, 2, HID])
        ex_u = sb("ex_u", [P, 2, HID])
        ex_h = sb("ex_h", [P, 3, HID])
        ex_hT = sb("ex_hT", [CH, 2, NCH, P])
        ex_y = sb("ex_y", [P, 3, DIM])
        bank = [ctx.enter_context(nc.psum_tensor(f"bank{i}", [P, 512], f32)) for i in range(5)]
        ps4 = ctx.enter_context(nc.psum_tensor("ps4", [P, 3, 512], f32))
        def B(i):
            return bank[i] if i < 5 else ps4[:, i - 5, :]

        x_in = [sem(f"x_in{h}") for h in range(HALVES)]
        raw_in, small_in, wgu_in, w2_in, zeroed = (sem(n) for n in ("raw_in", "small_in", "wgu_in", "w2_in", "zeroed"))
        consts, memsets, setup_ps, setup_sb, rates_sb, act_exp, toeplitz, masked = (
            sem(n) for n in ("consts", "memsets", "setup_ps", "setup_sb", "rates_sb", "act_exp", "toeplitz", "masked"))
        dve_a, dve_r, dve_b, dve_f = (sem(n) for n in ("dve_a", "dve_r", "dve_b", "dve_f"))
        a_norm, a_xT, a_mix, a_mixed, a_kvr, a_kmin, a_k, a_kv, a_gate = (
            sem(n) for n in ("a_norm", "a_xT", "a_mix", "a_mixed", "a_kvr", "a_kmin", "a_k", "a_kv", "a_gate"))
        a_wkv, a_den, a_rw, a_rT, a_rTs, a_out, a_x = (
            sem(n) for n in ("a_wkv", "a_den", "a_rw", "a_rT", "a_rTs", "a_out", "a_x"))
        r_norm, r_xT, r_xTs, r_dot, r_mask, r_count, r_gap, r_exp, r_routed, r_read = (
            sem(n) for n in ("r_norm", "r_xT", "r_xTs", "r_dot", "r_mask", "r_count", "r_gap", "r_exp", "r_routed",
                             "r_read"))
        e_xT, e_xTs, e_g, e_u, e_gb, e_silu, e_h, e_hT, e_hTs, e_y, e_yb = (
            sem(n) for n in ("e_xT", "e_xTs", "e_g", "e_u", "e_gb", "e_silu", "e_h", "e_hT", "e_hTs", "e_y", "e_yb"))
        e_ub = sem("e_ub")
        e_x_in = [sem(f"e_x_in{i}") for i in range(3)]
        e_y_out = [sem(f"e_y_out{i}") for i in range(3)]
        scattered, gathered, xn_free = sem("scattered"), sem("gathered"), sem("xn_free")
        b_norm, b_xT, b_xTs, b_qk, b_qks, b_sq, b_gram, b_ext, b_shift, b_exp, b_diag = (
            sem(n) for n in ("b_norm", "b_xT", "b_xTs", "b_qk", "b_qks", "b_sq", "b_gram", "b_ext", "b_shift",
                             "b_exp", "b_diag"))
        b_m, b_ms, b_p, b_pss, b_out, b_x = (sem(n) for n in ("b_m", "b_ms", "b_p", "b_pss", "b_out", "b_x"))
        f_done, stored = sem("f_done"), sem("stored")
        block = ctx.enter_context(nc.Block())

        def flat(ap):
            return ap.rearrange("p a d -> p (a d)")

        def rows(h, t, n=1):
            return X[:, bass.ds(h * TH + t, n), :]

        @block.sync
        def _(sp):
            sp.dma_start(X[:, 0:TH, :], x_tiles[:, 0:TH, :]).then_inc(x_in[0], 16)
            for n, name in enumerate(("Wk", "Wv", "Wr", "Wo")):
                sp.dma_start(raw[:, n, :], d["L0_attn_a_" + name]).then_inc(raw_in, 16)
            sp.dma_start(raw[:, 4:7, :], d["L0_attn_b_w_qkv"].rearrange("(n p) c -> p n c", p=P)).then_inc(raw_in, 16)
            sp.dma_start(raw[:, 7, :], d["L0_attn_b_w_out"]).then_inc(raw_in, 16)
            sp.dma_start(cent[:, :], d["L0_ffn_centroid"]).then_inc(raw_in, 16)
            sp.dma_start(X[:, TH:TILES, :], x_tiles[:, TH:TILES, :]).then_inc(x_in[1], 16)
            sp.wait_ge(memsets, 1)
            for buf in (sorted_x, sorted_y):
                zero_rows = buf.rearrange("(a p r) c -> a p (r c)", p=P, r=SLOT_TILES // 3)
                for a in range(6):
                    sp.dma_start(zero_rows[a], wgu[:, :, :, :].rearrange("p e n h -> p (e n h)")[:, 0:13 * DIM]
                                 ).then_inc(zeroed, 16)
            sp.wait_ge(zeroed, 16 * 12)
            sp.dma_start(wgu[:, :, 0, :], d["L0_ffn_Wg"].rearrange("e d h -> d e h")).then_inc(wgu_in, 16)
            sp.dma_start(wgu[:, :, 1, :], d["L0_ffn_W1"].rearrange("e d h -> d e h")).then_inc(wgu_in, 16)
            sp.dma_start(w2[:, :, :, :], d["L0_ffn_W2"].rearrange("e (c k) d -> k e c d", k=CH)).then_inc(w2_in, 16)
            sp.dma_start(bias_gu[:, :, 0, :], d["L0_ffn_bg"].partition_broadcast(P)).then_inc(wgu_in, 16)
            sp.dma_start(bias_gu[:, :, 1, :], d["L0_ffn_b1"].partition_broadcast(P)).then_inc(wgu_in, 16)
            sp.dma_start(bias_2[:, :, :], d["L0_ffn_b2"].partition_broadcast(P)).then_inc(w2_in, 16)

            def load(m, i, j):
                if not isinstance(i, int) or m * ALL_SLOT_TILES + i - 2 > 0:
                    sp.wait_ge(e_xT, m * ALL_SLOT_TILES + i - 2)
                if isinstance(i, int):
                    src = sorted_x[i * P:(i + 1) * P, :]
                else:
                    src = sorted_x[bass.ds(i * P, P), :]
                sp.dma_start(ex_x[:, j % 3, :], src).then_inc(e_x_in[j % 3], 16)

            def store(m, i, j):
                sp.wait_ge(e_yb, m * ALL_SLOT_TILES + i + 1)
                if isinstance(i, int):
                    dst = sorted_y[i * P:(i + 1) * P, :]
                else:
                    dst = sorted_y[bass.ds(i * P, P), :]
                sp.dma_start(dst, ex_y[:, j % 3, :]).then_inc(e_y_out[j % 3], 16)

            for m in range(2):
                def dispatched(h):
                    sp.wait_ge(scattered, 16 * 2 * TH * (2 * m + h + 1))
                dispatched(0)
                if m == 1:
                    sp.wait_ge(gathered, 16 * 2 * TH * HALVES)
                load(m, 0, 0)
                load(m, 1, 1)
                for i in range(0, UNROLL):
                    load(m, i + 2, i + 2)
                    if i >= 3:
                        store(m, i - 3, i - 3)
                split = SLOT_TILES // UNROLL
                with sp.Fori(1, split) as k:
                    for j in range(UNROLL):
                        load(m, k * UNROLL + (j + 2), j + 2)
                        store(m, k * UNROLL + (j - 3), j - 3)
                dispatched(1)
                with sp.Fori(split, ALL_SLOT_TILES // UNROLL - 1) as k:
                    for j in range(UNROLL):
                        load(m, k * UNROLL + (j + 2), j + 2)
                        store(m, k * UNROLL + (j - 3), j - 3)
                for i in range(ALL_SLOT_TILES - UNROLL, ALL_SLOT_TILES + 3):
                    if i + 2 < ALL_SLOT_TILES:
                        load(m, i + 2, i + 2)
                    store(m, i - 3, i - 3)
            for h in range(HALVES):
                sp.wait_ge(f_done, h + 1)
                sp.dma_start(out_tiles[:, h * TH:(h + 1) * TH, :], X[:, h * TH:(h + 1) * TH, :]).then_inc(stored, 16)
            sp.wait_ge(stored, 16 * HALVES)

        @block.gpsimd
        def _(pool):
            pool.memset(ones[:, :], 1.0)
            pool.memset(ident[:, :], 0.0)
            pool.memset(later[:, :], 0.0)
            pool.memset(same_head[:, :, :], 1.0)
            pool.memset(not_first[:, :, :], 1.0)
            pool.iota(lag[:, :], pattern=[[1, 2 * P]], base=-1, channel_multiplier=-1,
                      allow_small_or_imprecise_dtypes=True)
            pool.iota(rank[:, :, :], pattern=[[0, TH], [-1, EXPERTS]], base=EXPERTS, channel_multiplier=0,
                      allow_small_or_imprecise_dtypes=True)
            pool.iota(slot_no[:, :, :], pattern=[[1, SLOT_TILES], [0, EXPERTS]], base=0, channel_multiplier=0,
                      allow_small_or_imprecise_dtypes=True).then_inc(consts, 1)
            pool.wait_ge(consts, 1)
            pool.affine_select(out=ident[:, :], in_=ident[:, :], compare_op=ALU.not_equal, fill=1.0, base=0,
                               pattern=[[-1, P]], channel_multiplier=1)
            pool.affine_select(out=later[:, :], in_=later[:, :], compare_op=ALU.is_ge, fill=1.0, base=0,
                               pattern=[[-1, P]], channel_multiplier=1)
            pool.affine_select(out=not_first[:, :, :], in_=not_first[:, :, :], compare_op=ALU.not_equal, fill=0.0,
                               base=0, pattern=[[0, EXPERTS], [1, TH]], channel_multiplier=0)
            pool.affine_select(out=same_head[:, :, :], in_=same_head[:, :, :], compare_op=ALU.is_ge, fill=0.0,
                               base=0, pattern=[[-DH_B, HEADS_B], [0, DH_B]], channel_multiplier=1
                               ).then_inc(consts, 1)
            pool.wait_ge(consts, 2)
            pool.affine_select(out=same_head[:, :, :], in_=same_head[:, :, :], compare_op=ALU.is_ge, fill=0.0,
                               base=DH_B - 1, pattern=[[DH_B, HEADS_B], [0, DH_B]], channel_multiplier=-1
                               ).then_inc(consts, 1)

            def index(h, t, c):
                return slot_of[:, h, t, c:c + 1].bitcast(u32)

            pool.wait_ge(zeroed, 16 * 12)
            pool.sem_inc(xn_free, 1)
            for m in range(2):
                for h in range(HALVES):
                    r = 2 * m + h
                    pool.wait_ge(r_routed, r + 1)
                    for t in range(TH):
                        for c in range(2):
                            pool.indirect_dma_start(
                                out=sorted_x[:, :], out_offset=bass.IndirectOffsetOnAxis(ap=index(h, t, c), axis=0),
                                in_=xn_moe[:, t, :], in_offset=None).then_inc(scattered, 16)
                    pool.wait_ge(scattered, (r + 1) * 16 * 2 * TH)
                    pool.sem_inc(xn_free, 1)
                for h in range(HALVES):
                    r = 2 * m + h
                    for b in range(3):
                        pool.wait_ge(e_y_out[b], (r + 1) * (16 * SLOT_TILES // 3))
                    pool.wait_ge(b_x, r + 1)
                    for t in range(TH):
                        for c in range(2):
                            pool.indirect_dma_start(
                                out=picked[:, t, c, :], out_offset=None, in_=sorted_y[:, :],
                                in_offset=bass.IndirectOffsetOnAxis(ap=index(h, t, c), axis=0)).then_inc(gathered, 16)

        @block.scalar
        def _(act):
            act.dma_start(mixc[:, 0:1], d["L0_attn_a_time_mix"].rearrange("a b c -> c (a b)")).then_inc(small_in, 16)
            act.dma_start(mixc[:, 2:3], d["L0_attn_b_norm_weight"].rearrange("(c a) -> c a", a=1)
                          ).then_inc(small_in, 16)
            for i in range(HEADS_B):
                act.dma_start(mixc[i * DH_B:(i + 1) * DH_B, 3:4],
                              d["L0_attn_b_temperature"][i, :, 0].partition_broadcast(DH_B)).then_inc(small_in, 16)
            act.dma_start(rates[:, 0, :], d["L0_attn_a_time_decay"].rearrange("h a -> (h a)").partition_broadcast(P)
                          ).then_inc(small_in, 16)
            act.dma_start(rates[:, 1, :], d["L0_attn_a_time_first"].rearrange("h a -> (h a)").partition_broadcast(P)
                          ).then_inc(small_in, 16)
            act.wait_ge(small_in, 16 * (4 + HEADS_B))
            act.activation(rates[:, 2:4, :], rates[:, 0:2, :], ACT.Exp)
            act.activation(mixc[:, 3:4], mixc[:, 3:4], ACT.Exp).then_inc(act_exp, 1)
            act.wait_ge(rates_sb, 1)
            with act.Fori(0, HEADS_A) as i:
                act.activation(flat(decay[:, bass.ds(i, 1), :]), lag[:, :], ACT.Exp,
                               scale=rates[:, 2, bass.ds(i, 1)]).then_inc(toeplitz, 1)

            def rwkv_round(h):
                for g in range(GROUPS):
                    act.wait_ge(a_xT, h * GROUPS + g + 1)
                    if g >= 2:
                        act.wait_ge(a_kvr, h * GROUPS + g - 1)
                    act.activation(mixed[:, g % 2, :], B(g % 2)[:, :], ACT.Copy, scale=mixc[:, 0:1]
                                   ).then_inc(a_mix, 1)
                    act.wait_ge(a_kmin, h * GROUPS + g + 1)
                    for t in range(4):
                        kvr = B(2 + t)
                        last = act.activation(gate[:, 4 * g + t, :], kvr[:, 2 * DIM:3 * DIM], ACT.Copy)
                    act.activation(kv[:, 4 * g:4 * g + 4, 0, :], kmin[:, :, :], ACT.Exp).then_inc(a_k, 1)
                act.wait_ge(a_k, (h + 1) * GROUPS)
                last = act.activation(gate[:, :, :], gate[:, :, :], ACT.Sigmoid)
                last.then_inc(a_gate, 1)
                for n in range(8):
                    act.wait_ge(a_wkv, h * 8 + n + 1)
                    if n >= 2:
                        act.wait_ge(a_rw, h * 8 + n - 1)
                    heads = B(6 + n % 2)[:, :].rearrange("p (i b k c) -> p i b k c", i=4, b=BH, k=2)
                    act.activation(den[:, n % 2, :, :, :], heads[:, :, :, 0, :], ACT.Copy, bias=K_EPS
                                   ).then_inc(a_den, 1)
                for g in range(GROUPS):
                    act.wait_ge(a_rT, h * GROUPS + g + 1)
                    if g >= 2:
                        act.wait_ge(a_out, h * GROUPS + g - 1)
                    act.activation(yT[:, g % 2, :], B(g % 2)[:, :], ACT.Copy).then_inc(a_rTs, 1)

            def route_round(m, h):
                r = 2 * m + h
                for g in range(GROUPS):
                    act.wait_ge(r_xT, r * GROUPS + g + 1)
                    if g >= 2:
                        act.wait_ge(r_dot, r * GROUPS + g - 1)
                    act.activation(yT[:, g % 2, :], B(g % 2)[:, :], ACT.Copy).then_inc(r_xTs, 1)
                act.wait_ge(r_gap, r + 1)
                act.activation(far[:, 1, :], far[:, 0, :], ACT.Exp).then_inc(r_exp, 1)

            def expert_tile(m, i, j):
                base = m * ALL_SLOT_TILES
                first = isinstance(i, int)
                if not first or i + 1 < ALL_SLOT_TILES:
                    act.wait_ge(e_xT, base + i + 2)
                    if not first or base + i > 0:
                        act.wait_ge(e_u, base + i)
                    act.activation(ex_xT[:, (j + 1) % 2, :], B(0)[:, 0:P], ACT.Copy
                                   ).then_inc(e_xTs, 1)
                if not first or 0 <= i < ALL_SLOT_TILES:
                    act.wait_ge(e_gb, base + i + 1)
                    if not first or base + i > 1:
                        act.wait_ge(e_h, base + i - 1)
                    act.activation(ex_s[:, j % 2, :], ex_g[:, j % 2, :], ACT.Silu).then_inc(e_silu, 1)
                if not first or 0 <= i - 2 < ALL_SLOT_TILES:
                    act.wait_ge(e_hT, base + i - 1)
                    if not first or base + i > 3:
                        act.wait_ge(e_y, base + i - 3)
                    act.activation(ex_hT[:, j % 2, :, :], B(5 + j % 2)[0:CH, 0:NCH * P].rearrange(
                        "p (c t) -> p c t", c=NCH), ACT.Copy).then_inc(e_hTs, 1)

            def experts(m):
                for i in range(-1, UNROLL):
                    expert_tile(m, i, i)
                with act.Fori(1, ALL_SLOT_TILES // UNROLL - 1) as k:
                    for j in range(UNROLL):
                        expert_tile(m, k * UNROLL + j, j)
                for i in range(ALL_SLOT_TILES - UNROLL, ALL_SLOT_TILES + 3):
                    expert_tile(m, i, i)

            def channel_round(h):
                for g in range(GROUPS):
                    act.wait_ge(b_xT, h * GROUPS + g + 1)
                    act.activation(xT_half[:, 4 * g:4 * g + 4, :].rearrange("p t c -> p (t c)"), B(g % 2)[:, :],
                                   ACT.Copy, scale=mixc[:, 2:3]).then_inc(b_xTs, 1)
                    for s in range(2):
                        n = 2 * g + s
                        act.wait_ge(b_qk, h * BH + n + 1)
                        if n >= 2:
                            act.wait_ge(b_gram, h * BH + n - 1)
                        src = B(2 + s)[:, :].rearrange("p (t c) -> p t c", t=2)
                        act.activation(qk[:, s, :, :], src, ACT.Copy).then_inc(b_qks, 1)
                        act.activation(qk_sq[:, s, :, :], src, ACT.Square).then_inc(b_sq, 1)
                act.wait_ge(b_shift, h + 1)
                act.activation(att[:, :, :], att[:, :, :], ACT.Exp).then_inc(b_exp, 1)
                for g in range(2):
                    act.wait_ge(b_m, 2 * h + g + 1)
                    act.activation(folded[:, 0, :, :].rearrange("p b c -> p (b c)"), B(4)[:, :], ACT.Copy
                                   ).then_inc(b_ms, 1)
                    act.wait_ge(b_p, 2 * h + g + 1)
                    act.activation(folded[:, 1, :, :].rearrange("p b c -> p (b c)"), B(5)[:, :], ACT.Copy
                                   ).then_inc(b_pss, 1)

            with act.Fori(0, HALVES) as h:
                rwkv_round(h)
                route_round(0, h)
            experts(0)
            with act.Fori(0, HALVES) as h:
                channel_round(h)
                route_round(1, h)
            experts(1)

        @block.vector
        def _(dve):
            def rsqrt(ch, y, x, t):
                ch.step(dve.tensor_scalar(t.bitcast(i32), x.bitcast(i32), 1, None, ALU.arith_shift_right))
                ch.step(dve.tensor_scalar(y.bitcast(i32), t.bitcast(i32), -1.0, RSQRT_SEED, ALU.mult, ALU.add))
                for _ in range(4):
                    ch.step(dve.scalar_tensor_tensor(t, y, -0.5, y, ALU.mult, ALU.mult))
                    ch.step(dve.tensor_tensor(t, t, x, ALU.mult))
                    ch.step(dve.scalar_tensor_tensor(y, t, 1.5, y, ALU.add, ALU.mult))

            def layernorm(ch, h, dst, ready, rms):
                for t in range(TH):
                    last = dve.bn_stats(stats[:, t, :], flat(rows(h, t)))
                ch.step(last)
                dve.memset(carrier[:, :], 0.0)
                for t in range(TH):
                    last = dve.bn_aggr(mv[:, t, :], stats[:, t, :])
                ch.step(last)
                v, t0, t1 = mv[:, :, 1], small[:, 0, 0:TH], small[:, 1, 0:TH]
                ch.step(dve.tensor_scalar(t0, v, LN_EPS, None, ALU.add))
                rsqrt(ch, scale[:, :], t0, t1)
                if rms or rms is None:
                    ch.step(dve.tensor_tensor(t0, scale[:, :], scale[:, :], ALU.mult))
                    ch.step(dve.tensor_tensor(small[:, 3, 0:TH], t0, v, ALU.mult))
                if rms:
                    ch.step(dve.tensor_scalar(t0, small[:, 3, 0:TH], RMS_EPS, None, ALU.add))
                    rsqrt(ch, small[:, 2, 0:TH], t0, t1)
                    ch.step(dve.tensor_tensor(scale[:, :], scale[:, :], small[:, 2, 0:TH], ALU.mult))
                for t in range(TH):
                    last = dve.tensor_scalar(dst[:, t, :], flat(rows(h, t)), mv[:, t, 0:1], scale[:, t:t + 1],
                                             ALU.subtract, ALU.mult)
                    if t % 4 == 3:
                        last.then_inc(ready, 1)

            def rwkv_round(h):
                ch = Chain(dve, dve_a, h * A_STEPS, A_STEPS)
                layernorm(ch, h, xn, a_norm, False)
                for g in range(GROUPS):
                    dve.wait_ge(a_mix, h * GROUPS + g + 1)
                    m = mixed[:, g % 2, :].rearrange("p (b t) -> p b t", b=2)
                    dve.scalar_tensor_tensor(
                        m[:, :, 1:SEQ], B(g % 2)[:, :].rearrange("p (b t) -> p b t", b=2)[:, :, 0:SEQ - 1],
                        mixc[:, 1:2], m[:, :, 1:SEQ], ALU.mult, ALU.add).then_inc(a_mixed, 1)
                    dve.wait_ge(a_kvr, h * GROUPS + g + 1)
                    if g >= 1:
                        dve.wait_ge(a_k, h * GROUPS + g)
                    for t in range(4):
                        last = dve.tensor_scalar(kmin[:, t, :], B(2 + t)[:, 0:DIM], K_CLAMP, None, ALU.min)
                    last.then_inc(a_kmin, 1)
                    dve.wait_ge(a_k, h * GROUPS + g + 1)
                    for t in range(4):
                        last = dve.tensor_tensor(kv[:, 4 * g + t, 1, :], kv[:, 4 * g + t, 0, :],
                                                 B(2 + t)[:, DIM:2 * DIM], ALU.mult)
                    last.then_inc(a_kv, 1)
                dve.wait_ge(a_gate, h + 1)
                for n in range(8):
                    i, par = n // 2, n % 2
                    dve.wait_ge(a_den, h * 8 + n + 1)
                    if n >= 2:
                        dve.wait_ge(a_rw, h * 8 + n - 1)
                    ch.step(dve.reciprocal(rec[:, n % 2], den[:, n % 2, :, :, :]))
                    heads = B(6 + n % 2)[:, :].rearrange("p (i b k c) -> p i b k c", i=4, b=BH, k=2)
                    ch.step(dve.tensor_tensor(rec[:, n % 2], heads[:, :, :, 1, :], rec[:, n % 2], ALU.mult))
                    part = slice(32 * i, 32 * i + 32)
                    tiles = slice(par, TH, 2)
                    dve.tensor_tensor(
                        rwkv[:, tiles, part].rearrange("p b (i c) -> p i b c", i=4), rec[:, n % 2],
                        gate[:, tiles, part].rearrange("p b (i c) -> p i b c", i=4), ALU.mult).then_inc(a_rw, 1)
                for g in range(GROUPS):
                    dve.wait_ge(a_out, h * GROUPS + g + 1)
                    dve.tensor_tensor(rows(h, 4 * g, 4), rows(h, 4 * g, 4),
                                      B(6 + g % 2)[:, :].rearrange("p (t c) -> p t c", t=4), ALU.add
                                      ).then_inc(a_x, 1)
                dve.wait_ge(a_x, (h + 1) * GROUPS)
                ch.close()

            def wide(ap):
                return ap.unsqueeze(2).to_broadcast([P, TH, EXPERTS])

            def route_round(m, h):
                r = 2 * m + h
                ch = Chain(dve, dve_r, r * R_STEPS, R_STEPS)
                tt, ts, stt = dve.tensor_tensor, dve.tensor_scalar, dve.scalar_tensor_tensor
                dve.wait_ge(xn_free, r + 1)
                layernorm(ch, h, xn_moe, r_norm, None)
                dve.wait_ge(r_dot, (r + 1) * GROUPS)
                dot = B(2)[:, 0:TH * EXPERTS].rearrange("p (t e) -> p t e", t=TH)
                ch.step(stt(dist[:, :, :], dot, -2.0,
                            cent_sq[:, :].unsqueeze(1).to_broadcast([P, TH, EXPERTS]), ALU.mult, ALU.add))
                ch.step(ts(small[:, 2, 0:TH], small[:, 3, 0:TH], float(DIM), None, ALU.mult))
                ch.step(tt(dist[:, :, :], dist[:, :, :], wide(small[:, 2, 0:TH]), ALU.add))
                ch.step(ts(dist[:, :, :], dist[:, :, :], DIST_MIN, None, ALU.max))
                for c in range(2):
                    ch.step(dve.tensor_reduce(top[:, c, :], dist[:, :, :], AX.X, ALU.max))
                    ch.step(tt(t8[:, :, :], dist[:, :, :], wide(top[:, c, :]), ALU.is_equal))
                    ch.step(tt(t8[:, :, :], t8[:, :, :], rank[:, :, :], ALU.mult))
                    ch.step(dve.tensor_reduce(far[:, 0, :], t8[:, :, :], AX.X, ALU.max))
                    ch.step(tt(onehot[:, c, :, :], t8[:, :, :], wide(far[:, 0, :]), ALU.is_equal))
                    if c == 0:
                        ch.step(stt(dist[:, :, :], onehot[:, 0, :, :], -3.0e38, dist[:, :, :], ALU.mult, ALU.add))
                tt(mask[:, :, :], onehot[:, 0, :, :], onehot[:, 1, :, :], ALU.add).then_inc(r_mask, 1)
                rsqrt(ch, small[:, 0, 0:2 * TH], top[:, :, :].rearrange("p c t -> p (c t)"), small[:, 1, 0:2 * TH])
                ch.step(tt(small[:, 0, 0:2 * TH], small[:, 0, 0:2 * TH],
                           top[:, :, :].rearrange("p c t -> p (c t)"), ALU.mult))
                tt(far[:, 0, :], small[:, 0, TH:2 * TH], small[:, 0, 0:TH], ALU.subtract).then_inc(r_gap, 1)
                dve.wait_ge(r_count, r + 1)
                ch.step(dve.tensor_copy(counts[:, :, :], B(3)[:, 0:TH * EXPERTS].rearrange("p (t e) -> p e t", t=TH)))
                ch.step(dve.tensor_tensor_scan(upto[:, :, :].rearrange("p e t -> p (e t)"),
                                               not_first[:, :, :].rearrange("p e t -> p (e t)"),
                                               counts[:, :, :].rearrange("p e t -> p (e t)"), 0.0,
                                               ALU.mult, ALU.add))
                ch.step(ts(exp_i[:, :], upto[:, :, TH - 1], float(P - 1), None, ALU.add))
                ch.step(ts(exp_i[:, :], exp_i[:, :], P.bit_length() - 1, None, ALU.arith_shift_right))
                ch.step(dve.tensor_copy(exp_e[:, 0, :], exp_i[:, :]))
                ch.step(dve.tensor_tensor_scan(exp_e[:, 1, :], ones[:, 0:EXPERTS], exp_e[:, 0, :], 0.0,
                                               ALU.mult, ALU.add))
                ch.step(tt(exp_e[:, 2, :], exp_e[:, 1, :], exp_e[:, 0, :], ALU.subtract))
                ch.step(ts(exp_e[:, 2, :], exp_e[:, 2, :], float(P), None, ALU.mult))
                ch.step(tt(upto[:, :, :], upto[:, :, :], counts[:, :, :], ALU.subtract))
                ch.step(tt(upto[:, :, :], upto[:, :, :],
                           exp_e[:, 2, :].unsqueeze(2).to_broadcast([P, EXPERTS, TH]), ALU.add))
                ch.step(tt(dist[:, :, :], upto[:, :, :].rearrange("p e t -> p t e"),
                           B(4)[:, 0:TH * EXPERTS].rearrange("p (t e) -> p t e", t=TH), ALU.add))
                dve.sem_inc(r_read, 1)
                for c in range(2):
                    ch.step(tt(t8[:, :, :], dist[:, :, :], onehot[:, c, :, :], ALU.mult))
                    ch.step(dve.tensor_reduce(pos_f[:, :, c], t8[:, :, :], AX.X, ALU.add))
                half_slots = slot_of[:, bass.ds(h, 1), :, :].rearrange("p a t c -> p (a t c)")
                ch.step(ts(half_slots, pos_f[:, :, :].rearrange("p t c -> p (t c)"), half_base[:, bass.ds(h, 1)], None,
                           ALU.add))
                ch.step(tt(slot_cmp[:, :, :], slot_no[:, :, :],
                           exp_e[:, 1, :].unsqueeze(1).to_broadcast([P, SLOT_TILES, EXPERTS]), ALU.is_ge))
                ch.step(dve.tensor_reduce(slot_f[:, :], slot_cmp[:, :, :], AX.X, ALU.add))
                ts(expert_of[:, bass.ds(h * SLOT_TILES, SLOT_TILES)], slot_f[:, :], float(EXPERTS - 1), None,
                   ALU.min).then_inc(r_routed, 1)
                dve.wait_ge(r_exp, r + 1)
                ch.step(ts(top[:, 0, :], far[:, 1, :], 1.0, None, ALU.add))
                ch.step(dve.reciprocal(top[:, 1, :], top[:, 0, :]))
                both = weight[:, bass.ds(h, 1), :, :].rearrange("p a t c -> p (a t) c")
                dve.tensor_copy(both[:, :, 0], top[:, 1, :])
                ch.step(tt(both[:, :, 1], top[:, 1, :], far[:, 1, :], ALU.mult))
                ch.close()

            def expert_tile(m, i, j):
                base = m * ALL_SLOT_TILES
                first = isinstance(i, int)

                def expert_at(n):
                    ap = expert_of[0:1, n:n + 1] if isinstance(n, int) else expert_of[0:1, bass.ds(n, 1)]
                    return dve.value_load(ap, min_val=0, max_val=EXPERTS - 1)
                if not first or 0 <= i < ALL_SLOT_TILES:
                    e = expert_at(i)
                    dve.wait_ge(e_g, base + i + 1)
                    if not first or base + i > 1:
                        dve.wait_ge(e_silu, base + i - 1)
                    dve.tensor_tensor(ex_g[:, j % 2, :], B(1 + j % 2)[:, 0:HID], flat(bias_gu[:, bass.ds(e, 1), 0, :]),
                                      ALU.add).then_inc(e_gb, 1)
                    dve.wait_ge(e_u, base + i + 1)
                    if not first or base + i > 1:
                        dve.wait_ge(e_h, base + i - 1)
                    dve.tensor_tensor(ex_u[:, j % 2, :], B(3 + j % 2)[:, 0:HID], flat(bias_gu[:, bass.ds(e, 1), 1, :]),
                                      ALU.add).then_inc(e_ub, 1)
                    dve.wait_ge(e_ub, base + i + 1)
                    dve.wait_ge(e_silu, base + i + 1)
                    if not first or base + i > 2:
                        dve.wait_ge(e_hT, base + i - 2)
                    dve.tensor_tensor(ex_h[:, j % 3, :], ex_s[:, j % 2, :], ex_u[:, j % 2, :], ALU.mult
                                      ).then_inc(e_h, 1)
                if not first or 0 <= i - 3 < ALL_SLOT_TILES:
                    e = expert_at(i - 3)
                    dve.wait_ge(e_y, base + i - 2)
                    if not first or m > 0 or i >= 6:
                        n = (i - 3) // 3 if first else (i_third + (j - 3) // 3)
                        dve.wait_ge(e_y_out[j % 3], 16 * (m * ALL_SLOT_TILES // 3 + n) if first
                                    else n * 16 + 16 * (m * ALL_SLOT_TILES // 3))
                    dve.tensor_tensor(ex_y[:, j % 3, :], B(7)[:, 0:P],
                                      flat(bias_2[:, bass.ds(e, 1), :]), ALU.add).then_inc(e_yb, 1)

            def experts(m):
                nonlocal i_third
                for i in range(0, UNROLL):
                    expert_tile(m, i, i)
                with dve.Fori(1, ALL_SLOT_TILES // UNROLL - 1) as k:
                    i_third = k * (UNROLL // 3)
                    for j in range(UNROLL):
                        expert_tile(m, k * UNROLL + j, j)
                for i in range(ALL_SLOT_TILES - UNROLL, ALL_SLOT_TILES + 3):
                    expert_tile(m, i, i)

            def combine(ch, m, h):
                r = 2 * m + h
                dve.wait_ge(gathered, (r + 1) * (16 * 2 * TH))
                w = weight[:, bass.ds(h, 1), :, :].rearrange("p a t c -> p (a t) c")
                for c in range(2):
                    for t in range(TH):
                        last = dve.scalar_tensor_tensor(flat(rows(h, t)), picked[:, t, c, :], w[:, t, c:c + 1],
                                                        flat(rows(h, t)), ALU.mult, ALU.add)
                    ch.step(last)
                dve.sem_inc(b_x, 1)

            def channel_round(h):
                ch = Chain(dve, dve_b, h * B_STEPS, B_STEPS)
                tt, ts = dve.tensor_tensor, dve.tensor_scalar
                combine(ch, 0, h)
                layernorm(ch, h, xn, b_norm, True)
                for g in range(GROUPS):
                    dve.wait_ge(b_gram, h * BH + 2 * g + 2)
                    src = B(4 + g % 2)[:, :].rearrange("p (s k c) -> p s k c", s=2, k=2)
                    for s in range(2):
                        last = tt(gram[:, s, :, :, :].rearrange("p k a c -> p k (a c)"), src[:, s, :, :],
                                  same_head[:, :, :].rearrange("p a c -> p (a c)").unsqueeze(1).to_broadcast(
                                      [P, 2, P]), ALU.mult)
                    ch.step(last)
                    ch.step(dve.tensor_reduce(sims[:, 2 * g:2 * g + 2, :, :].rearrange("p s k c -> p (s k) c"),
                                              gram[:, :, :, :, :].rearrange("p s k a c -> p (s k) c a"), AX.X, ALU.add))
                    dve.sem_inc(b_ext, 1)
                ch.step(ts(qnorm[:, :], B(6)[:, 0:BH], 1e-24, None, ALU.max))
                rsqrt(ch, small[:, 2, 0:BH], qnorm[:, :], small[:, 1, 0:BH])
                ch.step(ts(small[:, 2, 0:BH], small[:, 2, 0:BH], mixc[:, 3:4], None, ALU.mult))
                knorm = small[:, 3, :]
                ch.step(ts(knorm.rearrange("p (b c) -> p b c", b=BH), sims[:, :, 1, :], 1e-24, None, ALU.max))
                rsqrt(ch, small[:, 0, :], knorm, small[:, 1, :])
                ch.step(tt(att[:, :, :], sims[:, :, 0, :], small[:, 0, :].rearrange("p (b c) -> p b c", b=BH),
                           ALU.mult))

                def row(ap):
                    return ap.unsqueeze(2).to_broadcast([P, BH, DH_B])
                ch.step(tt(att[:, :, :], att[:, :, :], row(small[:, 2, 0:BH]), ALU.mult))
                ch.step(dve.tensor_reduce(qnorm[:, :], att[:, :, :], AX.X, ALU.max))
                tt(att[:, :, :], att[:, :, :], row(qnorm[:, :]), ALU.subtract).then_inc(b_shift, 1)
                dve.wait_ge(b_exp, h + 1)
                ch.step(dve.tensor_reduce(qnorm[:, :], att[:, :, :], AX.X, ALU.add))
                ch.step(dve.reciprocal(small[:, 2, 0:BH], qnorm[:, :]))
                ch.step(tt(att[:, :, :], att[:, :, :], row(small[:, 2, 0:BH]), ALU.mult))
                for s in range(BH):
                    last = tt(att_diag[:, s, :, :], att[:, s, :].unsqueeze(1).to_broadcast([P, HEADS_B, DH_B]),
                              same_head[:, :, :], ALU.mult)
                last.then_inc(b_diag, 1)
                for g in range(GROUPS):
                    dve.wait_ge(b_out, h * GROUPS + g + 1)
                    tt(rows(h, 4 * g, 4), rows(h, 4 * g, 4), B(6 + g % 2)[:, :].rearrange("p (t c) -> p t c", t=4),
                       ALU.add).then_inc(a_x, 1)
                dve.wait_ge(a_x, h * GROUPS + GROUPS * (HALVES + 1))
                ch.close()

            i_third = None
            dve.memset(wgu[:, :, :, :].rearrange("p e n h -> p (e n h)")[:, 0:13 * DIM], 0.0).then_inc(memsets, 1)
            dve.memset(half_base[:, 0:1], 0.0)
            dve.memset(half_base[:, 1:2], float(SLOT_TILES * P))
            dve.wait_ge(consts, 3)
            dve.tensor_scalar(lag[:, :], lag[:, :], 0.0, None, ALU.max)
            dve.wait_ge(act_exp, 1)
            dve.tensor_scalar(mixc[:, 1:2], mixc[:, 0:1], -1.0, 1.0, ALU.mult, ALU.add)
            dve.tensor_scalar(rates[:, 2, :], rates[:, 2, :], -1.0, None, ALU.mult).then_inc(rates_sb, 1)
            dve.sem_inc(b_x, 1)
            dve.wait_ge(setup_ps, 1)
            dve.tensor_copy(wT[:, :, :].rearrange("p n c -> p (n c)"), B(0)[:, 0:3 * P])
            dve.tensor_copy(woT[:, :], B(0)[:, 3 * P:4 * P])
            dve.tensor_copy(wqkT[:, :, :].rearrange("p n c -> p (n c)"), B(1)[:, 0:2 * P])
            dve.tensor_copy(w_outT[:, :], B(1)[:, 2 * P:3 * P])
            dve.tensor_copy(centT[:, :], B(1)[:, 3 * P:3 * P + EXPERTS]).then_inc(setup_sb, 1)
            dve.wait_ge(setup_sb, 1)
            dve.tensor_tensor(centT2[:, :], centT[:, :], centT[:, :], ALU.mult).then_inc(setup_sb, 1)
            dve.wait_ge(setup_ps, 2)
            dve.tensor_copy(cent_sq[:, :], B(1)[:, 4 * P - EXPERTS:4 * P])
            with dve.Fori(0, HEADS_A) as i:
                dve.wait_ge(toeplitz, i + 1)
                diag = flat(decay[:, bass.ds(i, 1), 0:P])
                dve.tensor_tensor(diag, diag, later[:, :], ALU.mult).then_inc(masked, 1)
                dve.wait_ge(masked, 2 * i + 1)
                dve.scalar_tensor_tensor(diag, ident[:, :], rates[:, 3, bass.ds(i, 1)], diag, ALU.mult, ALU.add
                                         ).then_inc(masked, 1)
            dve.wait_ge(x_in[0], 16)
            dve.wait_ge(x_in[1], 16)
            with dve.Fori(0, HALVES) as h:
                rwkv_round(h)
                route_round(0, h)
            dve.wait_ge(wgu_in, 64)
            dve.wait_ge(w2_in, 32)
            experts(0)
            with dve.Fori(0, HALVES) as h:
                channel_round(h)
                route_round(1, h)
            experts(1)
            with dve.Fori(0, HALVES) as h:
                ch = Chain(dve, dve_f, h * F_STEPS, F_STEPS)
                combine(ch, 1, h)
                ch.close()
                dve.sem_inc(f_done, 1)

        @block.tensor
        def _(pe):
            def mm(o, l, r, start=True, stop=True):
                return pe.matmul(o, l, r, start=start, stop=stop)

            pe.wait_ge(consts, 3)
            pe.wait_ge(raw_in, 16 * 7)
            for n in range(4):
                pe.transpose(B(0)[:, n * P:(n + 1) * P], raw[:, n, :], ident[:, :])
            for n, w in enumerate((4, 5, 7)):
                pe.transpose(B(1)[:, n * P:(n + 1) * P], raw[:, w, :], ident[:, :])
            pe.transpose(B(1)[:, 3 * P:3 * P + EXPERTS], cent[:, :], ident[0:EXPERTS, 0:EXPERTS]
                         ).then_inc(setup_ps, 1)
            pe.wait_ge(setup_sb, 2)
            mm(B(1)[:, 4 * P - EXPERTS:4 * P], ones[:, :], centT2[:, :]).then_inc(setup_ps, 1)

            def rwkv_round(h):
                def transposes(g):
                    pe.wait_ge(a_norm, h * GROUPS + g + 1)
                    if g >= 2:
                        pe.wait_ge(a_mixed, h * GROUPS + g - 1)
                    for t in range(4):
                        last = pe.transpose(B(g % 2)[:, t * P:(t + 1) * P], xn[:, 4 * g + t, :], ident[:, :])
                    last.then_inc(a_xT, 1)
                transposes(0)
                for g in range(GROUPS):
                    if g + 1 < GROUPS:
                        transposes(g + 1)
                    pe.wait_ge(a_mixed, h * GROUPS + g + 1)
                    if g >= 1:
                        pe.wait_ge(a_k, h * GROUPS + g)
                        pe.wait_ge(a_kv, h * GROUPS + g)
                    for t in range(4):
                        last = mm(B(2 + t)[:, 0:3 * DIM], mixed[:, g % 2, t * P:(t + 1) * P],
                                  wT[:, :, :].rearrange("p n c -> p (n c)"))
                    last.then_inc(a_kvr, 1)
                pe.wait_ge(a_kv, (h + 1) * GROUPS)
                pe.wait_ge(masked, 2 * HEADS_A)
                for n in range(8):
                    i, par = n // 2, n % 2
                    if n >= 2:
                        pe.wait_ge(a_rw, h * 8 + n - 1)
                    for hd in range(4 * i, 4 * i + 4):
                        o = B(6 + n % 2)[:, (hd - 4 * i) * P:(hd - 4 * i + 1) * P]
                        cols = slice(DH_A * hd, DH_A * hd + DH_A)
                        if par == 0:
                            last = mm(o, decay[:, hd, 0:P], kv[:, 0:TH:2, :, cols])
                        else:
                            mm(o, decay[:, hd, P:2 * P], kv[:, 0:TH:2, :, cols], stop=False)
                            last = mm(o, decay[:, hd, 0:P], kv[:, 1:TH:2, :, cols], start=False)
                    last.then_inc(a_wkv, 1)
                pe.wait_ge(a_rw, (h + 1) * 8)

                def back(g):
                    if g >= 2:
                        pe.wait_ge(a_rTs, h * GROUPS + g - 1)
                    for t in range(4):
                        last = pe.transpose(B(g % 2)[:, t * P:(t + 1) * P], rwkv[:, 4 * g + t, :], ident[:, :])
                    last.then_inc(a_rT, 1)
                back(0)
                for g in range(GROUPS):
                    if g + 1 < GROUPS:
                        back(g + 1)
                    pe.wait_ge(a_rTs, h * GROUPS + g + 1)
                    if g >= 2:
                        pe.wait_ge(a_x, h * GROUPS + g - 1)
                    for t in range(4):
                        last = mm(B(6 + g % 2)[:, t * P:(t + 1) * P], yT[:, g % 2, t * P:(t + 1) * P], woT[:, :])
                    last.then_inc(a_out, 1)

            def route_round(m, h):
                r = 2 * m + h

                def transposes(g):
                    pe.wait_ge(r_norm, r * GROUPS + g + 1)
                    if g >= 2:
                        pe.wait_ge(r_xTs, r * GROUPS + g - 1)
                    for t in range(4):
                        last = pe.transpose(B(g % 2)[:, t * P:(t + 1) * P], xn_moe[:, 4 * g + t, :], ident[:, :])
                    last.then_inc(r_xT, 1)
                transposes(0)
                for g in range(GROUPS):
                    if g + 1 < GROUPS:
                        transposes(g + 1)
                    pe.wait_ge(r_xTs, r * GROUPS + g + 1)
                    for t in range(4):
                        c = (4 * g + t) * EXPERTS
                        last = mm(B(2)[:, c:c + EXPERTS], yT[:, g % 2, t * P:(t + 1) * P], centT[:, :])
                    last.then_inc(r_dot, 1)
                pe.wait_ge(r_mask, r + 1)
                chosen = mask[:, :, :].rearrange("p t e -> p (t e)")
                mm(B(3)[:, 0:TH * EXPERTS], ones[:, :], chosen)
                mm(B(4)[:, 0:TH * EXPERTS], later[:, :], chosen).then_inc(r_count, 1)

            def expert_tile(m, i, j):
                base = m * ALL_SLOT_TILES
                first = isinstance(i, int)

                def expert_at(n):
                    ap = expert_of[0:1, n:n + 1] if isinstance(n, int) else expert_of[0:1, bass.ds(n, 1)]
                    return pe.value_load(ap, min_val=0, max_val=EXPERTS - 1)
                if not first or i + 1 < ALL_SLOT_TILES:
                    if first:
                        pe.wait_ge(e_x_in[(i + 1) % 3], 16 * (m * ALL_SLOT_TILES // 3 + (i + 1) // 3 + 1))
                    else:
                        pe.wait_ge(e_x_in[(j + 1) % 3],
                                   i_third * 16 + 16 * (m * ALL_SLOT_TILES // 3 + (j + 1) // 3 + 1))
                    if not first or base + i + 1 > 0:
                        pe.wait_ge(e_xTs, base + i + 1)
                    pe.transpose(B(0)[:, 0:P], ex_x[:, (j + 1) % 3, :], ident[:, :]
                                 ).then_inc(e_xT, 1)
                if not first or 0 <= i < ALL_SLOT_TILES:
                    e = expert_at(i)
                    pe.wait_ge(e_xTs, base + i + 1)
                    if not first or base + i > 1:
                        pe.wait_ge(e_ub, base + i - 1)
                    mm(B(1 + j % 2)[:, 0:HID], ex_xT[:, j % 2, :], flat(wgu[:, bass.ds(e, 1), 0, :])).then_inc(e_g, 1)
                    mm(B(3 + j % 2)[:, 0:HID], ex_xT[:, j % 2, :], flat(wgu[:, bass.ds(e, 1), 1, :])).then_inc(e_u, 1)
                if not first or 0 <= i - 2 < ALL_SLOT_TILES:
                    pe.wait_ge(e_h, base + i - 1)
                    if not first or base + i > 3:
                        pe.wait_ge(e_hTs, base + i - 3)
                    for c in range(NCH):
                        last = pe.transpose(B(5 + j % 2)[0:CH, c * P:(c + 1) * P],
                                            ex_h[:, (j - 2) % 3, c * CH:(c + 1) * CH], ident[:, :])
                    last.then_inc(e_hT, 1)
                if not first or 0 <= i - 3 < ALL_SLOT_TILES:
                    e = expert_at(i - 3)
                    pe.wait_ge(e_hTs, base + i - 2)
                    if not first or base + i > 3:
                        pe.wait_ge(e_yb, base + i - 3)
                    for c in range(NCH):
                        last = mm(B(7)[:, 0:P], ex_hT[:, (j - 3) % 2, c, :],
                                  flat(w2[:, bass.ds(e, 1), c, :]), start=(c == 0), stop=(c == NCH - 1))
                    last.then_inc(e_y, 1)

            def experts(m):
                nonlocal i_third
                for i in range(-1, UNROLL):
                    expert_tile(m, i, i)
                with pe.Fori(1, ALL_SLOT_TILES // UNROLL - 1) as k:
                    i_third = k * (UNROLL // 3)
                    for j in range(UNROLL):
                        expert_tile(m, k * UNROLL + j, j)
                for i in range(ALL_SLOT_TILES - UNROLL, ALL_SLOT_TILES + 3):
                    expert_tile(m, i, i)

            def channel_round(h):
                def transposes(g):
                    pe.wait_ge(b_norm, h * GROUPS + g + 1)
                    if g >= 2:
                        pe.wait_ge(b_xTs, h * GROUPS + g - 1)
                    for t in range(4):
                        last = pe.transpose(B(g % 2)[:, t * P:(t + 1) * P], xn[:, 4 * g + t, :], ident[:, :])
                    last.then_inc(b_xT, 1)

                def qk_of(n):
                    pe.wait_ge(b_xTs, h * GROUPS + n // 2 + 1)
                    if n >= 2:
                        pe.wait_ge(b_sq, h * BH + n - 1)
                    for t in range(2):
                        last = mm(B(2 + n % 2)[:, t * 2 * P:(t + 1) * 2 * P], xT_half[:, 2 * n + t, :],
                                  wqkT[:, :, :].rearrange("p n c -> p (n c)"))
                    last.then_inc(b_qk, 1)

                def gram_of(n):
                    s, g = n % 2, n // 2
                    pe.wait_ge(b_sq, h * BH + n + 1)
                    if g >= 2 and s == 0:
                        pe.wait_ge(b_ext, h * GROUPS + g - 1)
                    o = B(4 + g % 2)[:, s * 2 * P:(s + 1) * 2 * P]
                    for t in range(2):
                        mm(o[:, 0:P], qk[:, s, t, 0:P], qk[:, s, t, P:2 * P], start=(t == 0), stop=(t == 1))
                    for t in range(2):
                        mm(o[:, P:2 * P], ones[:, :], qk_sq[:, s, t, P:2 * P], start=(t == 0), stop=(t == 1))
                    for t in range(2):
                        last = mm(B(6)[:, n:n + 1], qk_sq[:, s, t, 0:P], ones[:, 0:1], start=(t == 0), stop=(t == 1))
                    last.then_inc(b_gram, 1)
                transposes(0)
                qk_of(0)
                for g in range(GROUPS):
                    if g + 1 < GROUPS:
                        transposes(g + 1)
                    qk_of(2 * g + 1)
                    gram_of(2 * g)
                    if g + 1 < GROUPS:
                        qk_of(2 * g + 2)
                    gram_of(2 * g + 1)
                pe.wait_ge(b_diag, h + 1)
                for q in range(2):
                    if q == 1:
                        pe.wait_ge(b_ms, 2 * h + q)
                    for s in range(4):
                        last = mm(B(4)[:, s * P:(s + 1) * P],
                                  att_diag[:, 4 * q + s, :, :].rearrange("p a c -> p (a c)"), w_outT[:, :])
                    last.then_inc(b_m, 1)
                    pe.wait_ge(b_ms, 2 * h + q + 1)
                    mm(B(5)[:, :], raw[:, 6, :], folded[:, 0, :, :].rearrange("p b c -> p (b c)")).then_inc(b_p, 1)
                    pe.wait_ge(b_pss, 2 * h + q + 1)
                    for g in range(2 * q, 2 * q + 2):
                        if g >= 2:
                            pe.wait_ge(a_x, h * GROUPS + GROUPS * HALVES + g - 1)
                        for t in range(4):
                            last = mm(B(6 + g % 2)[:, t * P:(t + 1) * P], xT_half[:, 4 * g + t, :],
                                      folded[:, 1, 2 * (g % 2) + t // 2, :])
                        last.then_inc(b_out, 1)

            i_third = None
            with pe.Fori(0, HALVES) as h:
                rwkv_round(h)
                route_round(0, h)
            pe.wait_ge(wgu_in, 64)
            pe.wait_ge(w2_in, 32)
            pe.wait_ge(r_read, HALVES)
            experts(0)
            with pe.Fori(0, HALVES) as h:
                channel_round(h)
                route_round(1, h)
            pe.wait_ge(r_read, 2 * HALVES)
            experts(1)


_INS = ["L0_attn_a_x", "L0_attn_a_time_decay", "L0_attn_a_time_first", "L0_attn_a_time_mix", "L0_attn_a_Wk",
        "L0_attn_a_Wv", "L0_attn_a_Wr", "L0_attn_a_Wo", "L0_attn_b_norm_weight", "L0_attn_b_w_qkv",
        "L0_attn_b_temperature", "L0_attn_b_w_out", "L0_ffn_centroid", "L0_ffn_Wg", "L0_ffn_bg", "L0_ffn_W1",
        "L0_ffn_b1", "L0_ffn_W2", "L0_ffn_b2"]


def kernel(**inputs):
    import numpy as np
    import concourse.bacc as bacc
    from concourse.bass_utils import run_bass_kernel_spmd as run

    nc = bacc.Bacc("TRN2", target_bir_lowering=False, num_devices=1)
    arrays, aps = {}, {}
    for name in _INS:
        a = np.ascontiguousarray(inputs[name])
        arrays[f"in_{name}"] = a
        aps[name] = nc.dram_tensor(f"in_{name}", a.shape, mybir.dt.from_np(a.dtype), kind="ExternalInput").ap()
    out = nc.dram_tensor("out_0", (BATCH, SEQ, DIM), mybir.dt.float32, kind="ExternalOutput").ap()
    build(nc, aps, out)
    return run(nc, [arrays], core_ids=[0]).results[0]["out_0"]
```

```python
import concourse.bass as bass
from concourse import mybir
from contextlib import ExitStack

P = 128
BATCH, SEQ, DIM = 16, 256, 128
TOKENS = BATCH * SEQ
HALVES = 2
TILES = TOKENS // P
TH = TILES // HALVES
BH = BATCH // HALVES
GROUPS = TH // 4
HEADS_A, DH_A = 16, 8
HEADS_B, DH_B = 8, 16
EXPERTS, HID = 8, 342
CH, NCH = 114, 3
CHOICES = 2
SLOT_TILES = (TH * P * CHOICES + EXPERTS * (P - 1)) // P
ALL_SLOT_TILES = HALVES * SLOT_TILES
SLOTS = ALL_SLOT_TILES * P
UNROLL = 6
assert ALL_SLOT_TILES % UNROLL == 0 and SLOT_TILES % 3 == 0
LN_EPS, RMS_EPS, K_EPS, K_CLAMP, DIST_MIN = 1e-5, 1e-6, 1e-16, 60.0, 1e-12
RSQRT_SEED = float(0x5F3759DF)
A_STEPS, R_STEPS, B_STEPS, F_STEPS = 15, 63, 61, 8


class Chain:

    def __init__(self, eng, sem, start, per_round):
        self.eng, self.sem, self.start, self.per_round, self.n = eng, sem, start, per_round, 0

    def then(self, ins):
        ins.then_inc(self.sem, 1)
        self.n += 1
        return ins

    def wait(self):
        self.eng.wait_ge(self.sem, self.start + self.n)

    def step(self, ins):
        self.then(ins)
        self.wait()

    def close(self):
        assert self.n == self.per_round, (self.sem, self.n, self.per_round)


class Counts:

    def __init__(self, eng, start):
        self.eng, self.start, self.kept = eng, start, {}

    def __call__(self, n):
        if n not in self.kept:
            v = self.start + n
            self.kept[n] = v if isinstance(v, int) else self.eng.snap(v)
        return self.kept[n]


def wait_from(eng, sem, value):
    if not isinstance(value, int) or value > 0:
        eng.wait_ge(sem, value)


class Experts:

    def __init__(self, nc, eng, table, start):
        self.nc, self.eng, self.table, self.start, self.kept = nc, eng, table, start, {}

    def __call__(self, n):
        if n not in self.kept:
            at = self.start + n
            ap = self.table[0:1, at:at + 1] if isinstance(at, int) else self.table[0:1, bass.ds(at, 1)]
            self.kept[n] = self.nc.values_load(
                ap, engines=(self.eng.engine,), min_val=0, max_val=EXPERTS - 1,
                skip_runtime_bounds_check_because="the table is clamped to the experts when it is made")
        return self.kept[n]


def expert_loop(nc, eng, m, table, tile, first):
    base = m * ALL_SLOT_TILES

    def run(start, tiles, k=None):
        at = Counts(eng, start + base)
        if k is not None:
            at.third = Counts(eng, eng.snap(k * (16 * UNROLL // 3) + 16 * base // 3))
            at.round = Counts(eng, eng.snap(k * 16 + 16 * base // UNROLL))
        expert = Experts(nc, eng, table, start)
        for n in tiles:
            tile(n, at, expert)
    run(0, range(first, UNROLL))
    with eng.Fori(1, ALL_SLOT_TILES // UNROLL - 1) as k:
        run(eng.snap(k * UNROLL), range(UNROLL), k)
    run(0, range(ALL_SLOT_TILES - UNROLL, ALL_SLOT_TILES + 3))


ROUTE_PARTS = 7
ROUTE_AT_A = (0, 1, 2, 3, 4, 5)
ROUTE_AT_B = (1, 2, 3, 5, 6, 7)
COUNT_AT_A = 2


def build(nc, d, out):
    f32, i32, u32 = mybir.dt.float32, mybir.dt.int32, mybir.dt.uint32
    ACT, ALU, AX = mybir.ActivationFunctionType, mybir.AluOpType, mybir.AxisListType
    nc.disable_value_cache = True
    sorted_x = nc.dram_tensor("sorted_x", [SLOTS, DIM], f32, kind="Internal").ap()
    sorted_y = nc.dram_tensor("sorted_y", [SLOTS, DIM], f32, kind="Internal").ap()
    x_tiles = d["L0_attn_a_x"].rearrange("b (t p) d -> p (b t) d", p=P)
    out_tiles = out.rearrange("b (t p) d -> p (b t) d", p=P)
    with ExitStack() as ctx:
        def sb(name, shape, dt=f32):
            return ctx.enter_context(nc.sbuf_tensor(name, shape, dt))

        def sem(name):
            return ctx.enter_context(nc.semaphore(name))

        X = sb("X", [P, TILES, DIM])
        xn = sb("xn", [P, TH, DIM])
        xn_moe = sb("xn_moe", [P, TH, DIM])
        kv = sb("kv", [P, TH, 2, DIM])
        picked = kv
        gate = sb("gate", [P, TH, DIM])
        rwkv = sb("rwkv", [P, TH, DIM])
        xT_half = rwkv
        decay = sb("decay", [P, HEADS_A, 2 * P])
        wgu = sb("wgu", [P, EXPERTS, 2, HID])
        w2 = sb("w2", [CH, EXPERTS, NCH, DIM])
        bias_gu = sb("bias_gu", [P, EXPERTS, 2, HID])
        bias_2 = sb("bias_2", [P, EXPERTS, DIM])
        ident = sb("ident", [P, P])
        ones = sb("ones", [P, P])
        later = sb("later", [P, P])
        same_head = sb("same_head", [P, HEADS_B, DH_B])
        lag = sb("lag", [P, 2 * P])
        rank = sb("rank", [P, TH, EXPERTS])
        not_first = sb("not_first", [P, EXPERTS, TH])
        slot_no = sb("slot_no", [P, SLOT_TILES, EXPERTS])
        raw = sb("raw", [P, 8, DIM])
        cent = sb("cent", [EXPERTS, DIM])
        wT = sb("wT", [P, 3, DIM])
        woT = sb("woT", [P, DIM])
        wqkT = sb("wqkT", [P, 2, DIM])
        w_outT = sb("w_outT", [P, DIM])
        centT = sb("centT", [P, EXPERTS])
        centT2 = sb("centT2", [P, EXPERTS])
        cent_sq = sb("cent_sq", [P, EXPERTS])
        mixc = sb("mixc", [P, 4])
        rates = sb("rates", [P, 4, HEADS_A])
        mixed = sb("mixed", [P, 2, 4 * P])
        kmin = sb("kmin", [P, 2, 2, DIM])
        den = sb("den", [P, 2, 4, BH, DH_A])
        rec = sb("rec", [P, 3, 4, BH, DH_A])
        yT = sb("yT", [P, 2, 4 * P])
        stats = sb("stats", [P, TH, 6])
        mv = sb("mv", [P, TH, 2])
        scale = sb("scale", [P, 2, TH])
        shift = sb("shift", [P, 2, TH])
        small = sb("small", [P, 4, P])
        square = sb("square", [P, 4, 2 * TH])
        qk = gate[:, 0:8, :].rearrange("p (s t k) c -> p s t (k c)", s=2, t=2)
        qk_sq = gate[:, 8:16, :].rearrange("p (s t k) c -> p s t (k c)", s=2, t=2)
        gram = sb("gram", [P, 2, 2, HEADS_B, DH_B])
        sims = sb("sims", [P, BH, 2, DH_B])
        qnorm = sb("qnorm", [P, BH])
        att = sb("att", [P, BH, DH_B])
        att_diag = mixed[:, :, :].rearrange("p n (b a c) -> p (n b) a c", b=BH // 2, a=HEADS_B)
        folded = sb("folded", [P, 2, 4, DIM])
        dist = sb("dist", [P, TH, EXPERTS])
        t8 = sb("t8", [P, TH, EXPERTS])
        onehot = sb("onehot", [P, 2, TH, EXPERTS])
        mask = sb("mask", [P, TH, EXPERTS])
        counts = sb("counts", [P, EXPERTS, TH])
        upto = sb("upto", [P, EXPERTS, TH])
        top = sb("top", [P, 2, TH])
        far = sb("far", [P, 2, TH])
        pos_f = sb("pos_f", [P, TH, 2])
        exp_e = sb("exp_e", [P, 4, EXPERTS])
        exp_i = sb("exp_i", [P, EXPERTS], i32)
        carrier = sb("carrier", [P, 1])
        half_base = sb("half_base", [P, HALVES])
        slot_cmp = sb("slot_cmp", [P, SLOT_TILES, EXPERTS])
        slot_f = sb("slot_f", [P, SLOT_TILES])
        slot_of = sb("slot_of", [P, HALVES, TH, 2], i32)
        weight = sb("weight", [P, HALVES, TH, 2])
        expert_of = sb("expert_of", [P, ALL_SLOT_TILES], i32)
        ex_x = sb("ex_x", [P, UNROLL, DIM])
        ex_xT = sb("ex_xT", [P, 2, P])
        ex_g = sb("ex_g", [P, 2, HID])
        ex_s = sb("ex_s", [P, 2, HID])
        ex_u = sb("ex_u", [P, 2, HID])
        ex_h = sb("ex_h", [P, 3, HID])
        ex_hT = sb("ex_hT", [CH, 2, NCH, P])
        ex_y = sb("ex_y", [P, 3, DIM])
        banks = ctx.enter_context(nc.psum_tensor("banks", [P, 8, 512], f32))

        def B(i):
            return banks[:, i, :]

        def W(n):
            return banks[:, 2 + n % 6, :]

        def pair(n):
            return banks[:, 2 + 2 * (n % 2):4 + 2 * (n % 2), :]

        x_in = [sem(f"x_in{h}") for h in range(HALVES)]
        raw_in, small_in, wgu_in, w2_in, zeroed = (sem(n) for n in ("raw_in", "small_in", "wgu_in", "w2_in", "zeroed"))
        consts, memsets, setup_ps, setup_sb, rates_sb, act_exp, toeplitz, masked = (
            sem(n) for n in ("consts", "memsets", "setup_ps", "setup_sb", "rates_sb", "act_exp", "toeplitz", "masked"))
        dve_a, dve_r, dve_b, dve_f = (sem(n) for n in ("dve_a", "dve_r", "dve_b", "dve_f"))
        a_stats, r_stats, b_stats = (sem(n) for n in ("a_stats", "r_stats", "b_stats"))
        a_normv, r_normv, b_normv = (sem(n) for n in ("a_normv", "r_normv", "b_normv"))
        a_norm, a_xT, a_mix, a_mixed, a_kvr, a_kmin, a_k, a_kv, a_gate = (
            sem(n) for n in ("a_norm", "a_xT", "a_mix", "a_mixed", "a_kvr", "a_kmin", "a_k", "a_kv", "a_gate"))
        a_rec, a_ratio = sem("a_rec"), sem("a_ratio")
        a_wkv, a_den, a_rw, a_rT, a_rTs, a_out, a_x = (
            sem(n) for n in ("a_wkv", "a_den", "a_rw", "a_rT", "a_rTs", "a_out", "a_x"))
        r_norm, r_xT, r_xTs, r_dot, r_mask, r_count, r_gap, r_exp, r_routed, r_read = (
            sem(n) for n in ("r_norm", "r_xT", "r_xTs", "r_dot", "r_mask", "r_count", "r_gap", "r_exp", "r_routed",
                             "r_read"))
        e_xT, e_xTs, e_g, e_u, e_gb, e_silu, e_h, e_hT, e_hTs, e_y, e_yb = (
            sem(n) for n in ("e_xT", "e_xTs", "e_g", "e_u", "e_gb", "e_silu", "e_h", "e_hT", "e_hTs", "e_y", "e_yb"))
        e_ub = sem("e_ub")
        e_x_in = [sem(f"e_x_in{i}") for i in range(UNROLL)]
        e_y_out = [sem(f"e_y_out{i}") for i in range(3)]
        scattered, xn_free = sem("scattered"), sem("xn_free")
        gathered = [sem(f"gathered{g}") for g in range(GROUPS)]
        b_norm, b_xT, b_xTs, b_qk, b_qks, b_sq, b_gram, b_ext, b_shift, b_exp, b_diag = (
            sem(n) for n in ("b_norm", "b_xT", "b_xTs", "b_qk", "b_qks", "b_sq", "b_gram", "b_ext", "b_shift",
                             "b_exp", "b_diag"))
        b_m, b_ms, b_p, b_pss, b_out, b_x = (sem(n) for n in ("b_m", "b_ms", "b_p", "b_pss", "b_out", "b_x"))
        b_rows = sem("b_rows")
        f_done, stored, channel_in = sem("f_done"), sem("stored"), sem("channel_in")
        block = ctx.enter_context(nc.Block())

        def flat(ap):
            return ap.rearrange("p a d -> p (a d)")

        def rows(h, t, n=1):
            return X[:, h * TH + t:h * TH + t + n, :]

        @block.sync
        def _(sp):
            sp.dma_start(X[:, 0:TH, :], x_tiles[:, 0:TH, :]).then_inc(x_in[0], 16)
            for n, name in enumerate(("Wk", "Wv", "Wr", "Wo")):
                sp.dma_start(raw[:, n, :], d["L0_attn_a_" + name]).then_inc(raw_in, 16)
            sp.dma_start(raw[:, 4:7, :], d["L0_attn_b_w_qkv"].rearrange("(n p) c -> p n c", p=P)).then_inc(raw_in, 16)
            sp.dma_start(raw[:, 7, :], d["L0_attn_b_w_out"]).then_inc(raw_in, 16)
            sp.dma_start(cent[:, :], d["L0_ffn_centroid"]).then_inc(raw_in, 16)
            sp.dma_start(X[:, TH:TILES, :], x_tiles[:, TH:TILES, :]).then_inc(x_in[1], 16)
            sp.wait_ge(memsets, 1)
            for buf in (sorted_x, sorted_y):
                zero_rows = buf.rearrange("(a p r) c -> a p (r c)", p=P, r=SLOT_TILES // 3)
                for a in range(6):
                    sp.dma_start(zero_rows[a], wgu[:, :, :, :].rearrange("p e n h -> p (e n h)")[:, 0:13 * DIM]
                                 ).then_inc(zeroed, 16)
            sp.wait_ge(zeroed, 16 * 12)
            sp.dma_start(wgu[:, :, 0, :], d["L0_ffn_Wg"].rearrange("e d h -> d e h")).then_inc(wgu_in, 16)
            sp.dma_start(wgu[:, :, 1, :], d["L0_ffn_W1"].rearrange("e d h -> d e h")).then_inc(wgu_in, 16)
            sp.dma_start(w2[:, :, :, :], d["L0_ffn_W2"].rearrange("e (c k) d -> k e c d", k=CH)).then_inc(w2_in, 16)
            sp.dma_start(bias_gu[:, :, 0, :], d["L0_ffn_bg"].partition_broadcast(P)).then_inc(wgu_in, 16)
            sp.dma_start(bias_gu[:, :, 1, :], d["L0_ffn_b1"].partition_broadcast(P)).then_inc(wgu_in, 16)
            sp.dma_start(bias_2[:, :, :], d["L0_ffn_b2"].partition_broadcast(P)).then_inc(w2_in, 16)

            sp.dma_start(mixc[:, 2:3], d["L0_attn_b_norm_weight"].rearrange("(c a) -> c a", a=1)
                         ).then_inc(channel_in, 16)
            for i in range(HEADS_B):
                sp.dma_start(mixc[i * DH_B:(i + 1) * DH_B, 3:4],
                             d["L0_attn_b_temperature"][i, :, 0].partition_broadcast(DH_B)).then_inc(channel_in, 16)

            def load(i, start, at):
                wait_from(sp, e_xT, at(i - UNROLL + 1))
                src = bass.ds(start * P + i * P, P) if not isinstance(start, int) else slice(i * P, (i + 1) * P)
                sp.dma_start(ex_x[:, i % UNROLL, :], sorted_x[src, :]).then_inc(e_x_in[i % UNROLL], 16)

            def store(i, start, at):
                sp.wait_ge(e_yb, at(i + 1))
                dst = bass.ds(start * P + i * P, P) if not isinstance(start, int) else slice(i * P, (i + 1) * P)
                sp.dma_start(sorted_y[dst, :], ex_y[:, i % 3, :]).then_inc(e_y_out[i % 3], 16)

            split = SLOT_TILES // UNROLL
            ahead = SLOT_TILES - split * UNROLL
            assert 2 <= ahead < UNROLL
            for m in range(2):
                def run(start, tiles):
                    at = Counts(sp, start + m * ALL_SLOT_TILES)
                    for i in tiles:
                        if not isinstance(start, int) or i + ahead < ALL_SLOT_TILES:
                            load(i + ahead, start, at)
                        if not isinstance(start, int) or i >= 3:
                            store(i - 3, start, at)
                sp.wait_ge(scattered, 16 * 2 * TH * (2 * m + 1))
                for i in range(ahead):
                    load(i, 0, Counts(sp, m * ALL_SLOT_TILES))
                run(0, range(UNROLL))
                with sp.Fori(1, split) as k:
                    run(sp.snap(k * UNROLL), range(UNROLL))
                sp.wait_ge(scattered, 16 * 2 * TH * (2 * m + 2))
                with sp.Fori(split, ALL_SLOT_TILES // UNROLL - 1) as k:
                    run(sp.snap(k * UNROLL), range(UNROLL))
                run(0, range(ALL_SLOT_TILES - UNROLL, ALL_SLOT_TILES + 3))
            for g in range(HALVES * GROUPS):
                sp.wait_ge(f_done, g + 1)
                sp.dma_start(out_tiles[:, 4 * g:4 * g + 4, :], X[:, 4 * g:4 * g + 4, :]).then_inc(stored, 16)
            sp.wait_ge(stored, 16 * HALVES * GROUPS)

        @block.gpsimd
        def _(pool):
            pool.memset(ones[:, :], 1.0)
            pool.memset(ident[:, :], 0.0)
            pool.memset(later[:, :], 0.0)
            pool.memset(same_head[:, :, :], 1.0)
            pool.memset(not_first[:, :, :], 1.0)
            pool.iota(lag[:, :], pattern=[[1, 2 * P]], base=-1, channel_multiplier=-1,
                      allow_small_or_imprecise_dtypes=True)
            pool.iota(rank[:, :, :], pattern=[[0, TH], [-1, EXPERTS]], base=EXPERTS, channel_multiplier=0,
                      allow_small_or_imprecise_dtypes=True)
            pool.iota(slot_no[:, :, :], pattern=[[1, SLOT_TILES], [0, EXPERTS]], base=0, channel_multiplier=0,
                      allow_small_or_imprecise_dtypes=True).then_inc(consts, 1)
            pool.wait_ge(consts, 1)
            pool.affine_select(out=ident[:, :], in_=ident[:, :], compare_op=ALU.not_equal, fill=1.0, base=0,
                               pattern=[[-1, P]], channel_multiplier=1)
            pool.affine_select(out=later[:, :], in_=later[:, :], compare_op=ALU.is_ge, fill=1.0, base=0,
                               pattern=[[-1, P]], channel_multiplier=1)
            pool.affine_select(out=not_first[:, :, :], in_=not_first[:, :, :], compare_op=ALU.not_equal, fill=0.0,
                               base=0, pattern=[[0, EXPERTS], [1, TH]], channel_multiplier=0)
            pool.affine_select(out=same_head[:, :, :], in_=same_head[:, :, :], compare_op=ALU.is_ge, fill=0.0,
                               base=0, pattern=[[-DH_B, HEADS_B], [0, DH_B]], channel_multiplier=1
                               ).then_inc(consts, 1)
            pool.wait_ge(consts, 2)
            pool.affine_select(out=same_head[:, :, :], in_=same_head[:, :, :], compare_op=ALU.is_ge, fill=0.0,
                               base=DH_B - 1, pattern=[[DH_B, HEADS_B], [0, DH_B]], channel_multiplier=-1
                               ).then_inc(consts, 1)

            pool.wait_ge(act_exp, 1)
            diagonal = rwkv[:, :, :]
            pool.tensor_tensor(diagonal, ident[:, :].unsqueeze(1).to_broadcast([P, HEADS_A, P]),
                               rates[:, 3, :].unsqueeze(2).to_broadcast([P, HEADS_A, P]), ALU.mult)
            pool.wait_ge(toeplitz, HEADS_A)
            pool.affine_select(out=decay[:, :, 0:P], in_=decay[:, :, 0:P], compare_op=ALU.is_gt, fill=0.0, base=0,
                               pattern=[[0, HEADS_A], [1, P]], channel_multiplier=-1).then_inc(masked, 1)
            pool.wait_ge(masked, 1)
            pool.tensor_tensor(decay[:, :, 0:P], decay[:, :, 0:P], diagonal, ALU.add).then_inc(masked, 1)
            def index(h, t, c):
                return slot_of[:, h, t, c:c + 1].bitcast(u32)

            pool.wait_ge(zeroed, 16 * 12)
            pool.sem_inc(xn_free, 1)

            def gate_rows(h, n):
                i, par = n // 2, n % 2
                part, tiles = slice(32 * i, 32 * i + 32), slice(par, TH, 2)
                pool.wait_ge(a_ratio, h * 8 + n + 1)
                pool.tensor_tensor(
                    rwkv[:, tiles, part].rearrange("p b (i c) -> p i b c", i=4), rec[:, n % 3],
                    gate[:, tiles, part].rearrange("p b (i c) -> p i b c", i=4), ALU.mult).then_inc(a_rw, 1)
            for n in range(8):
                gate_rows(0, n)
            for m in range(2):
                for h in range(HALVES):
                    r = 2 * m + h
                    pool.wait_ge(r_routed, r + 1)
                    for t in range(TH):
                        if r == 0 and 5 <= t < 8 + 5:
                            gate_rows(1, t - 5)
                        for c in range(2):
                            pool.indirect_dma_start(
                                out=sorted_x[:, :], out_offset=bass.IndirectOffsetOnAxis(ap=index(h, t, c), axis=0),
                                in_=xn_moe[:, t, :], in_offset=None).then_inc(scattered, 16)
                    pool.wait_ge(scattered, (r + 1) * 16 * 2 * TH)
                    pool.sem_inc(xn_free, 1)
                for h in range(HALVES):
                    r = 2 * m + h
                    for b in range(3):
                        pool.wait_ge(e_y_out[b], (r + 1) * (16 * SLOT_TILES // 3))
                    pool.wait_ge(b_x, r + 1)
                    for t in range(TH):
                        for c in range(2):
                            pool.indirect_dma_start(
                                out=picked[:, t, c, :], out_offset=None, in_=sorted_y[:, :],
                                in_offset=bass.IndirectOffsetOnAxis(ap=index(h, t, c), axis=0)
                                ).then_inc(gathered[t // 4], 16)

        @block.scalar
        def _(act):
            act.dma_start(mixc[:, 0:1], d["L0_attn_a_time_mix"].rearrange("a b c -> c (a b)")).then_inc(small_in, 16)
            act.dma_start(rates[:, 0, :], d["L0_attn_a_time_decay"].rearrange("h a -> (h a)").partition_broadcast(P)
                          ).then_inc(small_in, 16)
            act.dma_start(rates[:, 1, :], d["L0_attn_a_time_first"].rearrange("h a -> (h a)").partition_broadcast(P)
                          ).then_inc(small_in, 16)
            act.wait_ge(small_in, 16 * 3)
            act.activation(rates[:, 2:4, :], rates[:, 0:2, :], ACT.Exp).then_inc(act_exp, 1)

            def normalise(h, dst, k, stats_ready, count, ready):
                act.wait_ge(stats_ready, count)
                for t in range(TH // 2, TH):
                    last = act.activation(dst[:, t, :], X[:, h * TH + t, :], ACT.Identity, scale=scale[:, k, t:t + 1],
                                          bias=shift[:, k, t:t + 1])
                    if t % 4 == 3:
                        last.then_inc(ready, 1)

            def rwkv_round(h):
                def mix(g):
                    act.wait_ge(a_xT, h * GROUPS + g + 1)
                    if g >= 2:
                        act.wait_ge(a_kvr, h * BH + 2 * (g - 1))
                    act.activation(mixed[:, g % 2, :], B(g % 2)[:, :], ACT.Copy, scale=mixc[:, 0:1]
                                   ).then_inc(a_mix, 1)
                normalise(h, xn, 0, a_stats, h + 1, a_norm)
                if h == 0:
                    act.wait_ge(rates_sb, 1)
                mix(0)
                mix(1)
                for n in range(BH):
                    act.wait_ge(a_kmin, h * BH + n + 1)
                    act.activation(kv[:, 2 * n:2 * n + 2, 0, :], kmin[:, n % 2, :, :], ACT.Exp)
                    act.activation(gate[:, 2 * n:2 * n + 2, :], pair(n)[:, :, 2 * DIM:3 * DIM], ACT.Copy
                                   ).then_inc(a_k, 1)
                    if h == 0 and n < HEADS_A // 4:
                        for i in range(4 * n, 4 * n + 4):
                            act.activation(decay[:, i, :], lag[:, :], ACT.Exp, scale=rates[:, 2, i:i + 1]
                                           ).then_inc(toeplitz, 1)
                    if h == 1 and n == 2:
                        gap_exp(0, 0)
                    if n % 2 == 1 and n // 2 + 2 < GROUPS:
                        mix(n // 2 + 2)
                act.wait_ge(a_k, (h + 1) * BH)
                act.activation(gate[:, :, :], gate[:, :, :], ACT.Sigmoid).then_inc(a_gate, 1)
                for n in range(8):
                    act.wait_ge(a_wkv, h * 8 + n + 1)
                    if n >= 2:
                        act.wait_ge(a_rec, h * 8 + n - 1)
                    heads = W(n)[:, :].rearrange("p (i b k c) -> p i b k c", i=4, b=BH, k=2)
                    act.activation(den[:, n % 2, :, :, :], heads[:, :, :, 0, :], ACT.Copy, bias=K_EPS
                                   ).then_inc(a_den, 1)
                for g in range(GROUPS):
                    act.wait_ge(a_rT, h * GROUPS + g + 1)
                    if g >= 2:
                        act.wait_ge(a_out, h * GROUPS + g - 1)
                    act.activation(yT[:, g % 2, :], B(g % 2)[:, :], ACT.Copy).then_inc(a_rTs, 1)

            def route_round(m, h):
                r = 2 * m + h
                act.wait_ge(xn_free, r + 1)
                normalise(h, xn_moe, 1, r_stats, r + 1, r_norm)
                for g in range(GROUPS):
                    act.wait_ge(r_xT, r * GROUPS + g + 1)
                    if g >= 2:
                        act.wait_ge(r_dot, r * GROUPS + g - 1)
                    act.activation(yT[:, g % 2, :], B(g % 2)[:, :], ACT.Copy).then_inc(r_xTs, 1)

            def gap_exp(m, h):
                act.wait_ge(r_gap, 2 * m + h + 1)
                act.activation(far[:, 1, :], far[:, 0, :], ACT.Exp).then_inc(r_exp, 1)

            def expert_tile(i, at, expert):
                live = isinstance(at.start, int)
                if not live or i + 1 < ALL_SLOT_TILES:
                    act.wait_ge(e_xT, at(i + 2))
                    act.activation(ex_xT[:, (i + 1) % 2, :], B(0)[:, 0:P], ACT.Copy).then_inc(e_xTs, 1)
                if not live or 0 <= i < ALL_SLOT_TILES:
                    act.wait_ge(e_gb, at(i + 1))
                    act.activation(ex_s[:, i % 2, :], ex_g[:, i % 2, :], ACT.Silu).then_inc(e_silu, 1)
                if not live or 0 <= i - 2 < ALL_SLOT_TILES:
                    act.wait_ge(e_hT, at(i - 1))
                    act.activation(ex_hT[:, i % 2, :, :], B(5 + i % 2)[0:CH, 0:NCH * P].rearrange(
                        "p (c t) -> p c t", c=NCH), ACT.Copy).then_inc(e_hTs, 1)

            def channel_round(h):
                normalise(h, xn, 0, b_stats, h + 1, b_norm)
                for g in range(GROUPS):
                    act.wait_ge(b_xT, h * GROUPS + g + 1)
                    act.activation(xT_half[:, 4 * g:4 * g + 4, :].rearrange("p t c -> p (t c)"), B(g % 2)[:, :],
                                   ACT.Copy, scale=mixc[:, 2:3]).then_inc(b_xTs, 1)
                    for s in range(2):
                        n = 2 * g + s
                        act.wait_ge(b_qks, h * BH + n + 1)
                        act.activation(qk_sq[:, s, :, :], qk[:, s, :, :], ACT.Square).then_inc(b_sq, 1)
                    if h == 1 and g == 2:
                        gap_exp(1, 0)
                act.wait_ge(b_shift, h + 1)
                act.activation(att[:, :, :], att[:, :, :], ACT.Exp).then_inc(b_exp, 1)
                for g in range(2):
                    act.wait_ge(b_m, 2 * h + g + 1)
                    act.activation(folded[:, 0, :, :].rearrange("p b c -> p (b c)"), B(4)[:, :], ACT.Copy
                                   ).then_inc(b_ms, 1)
                    act.wait_ge(b_p, 2 * h + g + 1)
                    act.activation(folded[:, 1, :, :].rearrange("p b c -> p (b c)"), B(5)[:, :], ACT.Copy
                                   ).then_inc(b_pss, 1)

            for h in range(HALVES):
                rwkv_round(h)
                route_round(0, h)
            gap_exp(0, 1)
            expert_loop(nc, act, 0, expert_of, expert_tile, -1)
            act.wait_ge(channel_in, 16 * (1 + HEADS_B))
            act.activation(mixc[:, 3:4], mixc[:, 3:4], ACT.Exp)
            for h in range(HALVES):
                channel_round(h)
                route_round(1, h)
            gap_exp(1, 1)
            expert_loop(nc, act, 1, expert_of, expert_tile, -1)

        @block.vector
        def _(dve):
            def rsqrt(ch, y, x, t):
                ch.step(dve.tensor_scalar(t.bitcast(i32), x.bitcast(i32), 1, None, ALU.arith_shift_right))
                ch.step(dve.tensor_scalar(y.bitcast(i32), t.bitcast(i32), -1.0, RSQRT_SEED, ALU.mult, ALU.add))
                for _ in range(3):
                    ch.step(dve.scalar_tensor_tensor(t, y, -0.5, y, ALU.mult, ALU.mult))
                    ch.step(dve.tensor_tensor(t, t, x, ALU.mult))
                    ch.step(dve.scalar_tensor_tensor(y, t, 1.5, y, ALU.add, ALU.mult))

            def row_stats(h, g):
                for t in range(4 * g, 4 * g + 4):
                    last = dve.bn_stats(stats[:, t, :], X[:, h * TH + t, :])
                return last

            def layernorm(ch, h, k, ready, dst, done, rms=False, mean_square=None, fresh=False):
                for g in range(GROUPS if fresh else 0):
                    last = row_stats(h, g)
                if fresh:
                    ch.step(last)
                for t in range(TH):
                    last = dve.bn_aggr(mv[:, t, :], stats[:, t, :])
                ch.step(last)
                v, t0, t1 = mv[:, :, 1], small[:, 0, 0:TH], small[:, 1, 0:TH]
                if rms:
                    ch.step(dve.tensor_scalar(t0, v, 1.0 + RMS_EPS, LN_EPS * RMS_EPS, ALU.mult, ALU.add))
                else:
                    ch.step(dve.tensor_scalar(t0, v, LN_EPS, None, ALU.add))
                rsqrt(ch, scale[:, k, :], t0, t1)
                dve.scalar_tensor_tensor(shift[:, k, :], mv[:, :, 0], -1.0, scale[:, k, :], ALU.mult, ALU.mult
                                         ).then_inc(ready, 1)
                for t in range(TH // 2):
                    last = dve.tensor_scalar(dst[:, t, :], X[:, h * TH + t, :], mv[:, t, 0:1],
                                             scale[:, k, t:t + 1],
                                             ALU.subtract, ALU.mult)
                    if t % 4 == 3:
                        last.then_inc(done, 1)
                if mean_square is not None:
                    ch.step(dve.tensor_tensor(t0, scale[:, k, :], scale[:, k, :], ALU.mult))
                    ch.step(dve.tensor_tensor(mean_square, t0, v, ALU.mult))

            def add_rows(ch, h, before, arrived, arrived_before):
                for g in range(GROUPS):
                    dve.wait_ge(arrived, arrived_before + g + 1)
                    dve.tensor_tensor(rows(h, 4 * g, 4), rows(h, 4 * g, 4),
                                      B(6 + g % 2)[:, :].rearrange("p (t c) -> p t c", t=4), ALU.add
                                      ).then_inc(a_x, 1)
                    if g >= 1:
                        dve.wait_ge(a_x, before + g)
                        row_stats(h, g - 1)
                dve.wait_ge(a_x, before + GROUPS)
                ch.step(row_stats(h, GROUPS - 1))

            def setup_weights():
                dve.wait_ge(setup_ps, 1)
                dve.tensor_copy(wT[:, :, :].rearrange("p n c -> p (n c)"), B(6)[:, 0:3 * P])
                dve.tensor_copy(woT[:, :], B(6)[:, 3 * P:4 * P])
                dve.tensor_copy(wqkT[:, :, :].rearrange("p n c -> p (n c)"), B(7)[:, 0:2 * P])
                dve.tensor_copy(w_outT[:, :], B(7)[:, 2 * P:3 * P])
                dve.tensor_copy(centT[:, :], B(7)[:, 3 * P:3 * P + EXPERTS]).then_inc(setup_sb, 1)
                dve.wait_ge(setup_sb, 1)
                dve.tensor_tensor(centT2[:, :], centT[:, :], centT[:, :], ALU.mult).then_inc(setup_sb, 1)
                dve.wait_ge(setup_ps, 2)
                dve.tensor_copy(cent_sq[:, :], B(7)[:, 4 * P - EXPERTS:4 * P])

            def rwkv_round(h):
                ch = Chain(dve, dve_a, h * A_STEPS, A_STEPS)

                def mix(g):
                    dve.wait_ge(a_mix, h * GROUPS + g + 1)
                    m = mixed[:, g % 2, :].rearrange("p (b t) -> p b t", b=2)
                    dve.scalar_tensor_tensor(
                        m[:, :, 1:SEQ], B(g % 2)[:, :].rearrange("p (b t) -> p b t", b=2)[:, :, 0:SEQ - 1],
                        mixc[:, 1:2], m[:, :, 1:SEQ], ALU.mult, ALU.add).then_inc(a_mixed, 1)

                def times_v(n):
                    dve.wait_ge(a_k, h * BH + n + 1)
                    dve.tensor_tensor(kv[:, 2 * n:2 * n + 2, 1, :], kv[:, 2 * n:2 * n + 2, 0, :],
                                      pair(n)[:, :, DIM:2 * DIM], ALU.mult).then_inc(a_kv, 1)
                dve.wait_ge(x_in[h], 16)
                layernorm(ch, h, 0, a_stats, xn, a_normv, fresh=True)
                if h == 0:
                    setup_weights()
                    dve.wait_ge(consts, 3)
                    dve.tensor_scalar(lag[:, :], lag[:, :], 0.0, None, ALU.max)
                    dve.wait_ge(act_exp, 1)
                    dve.tensor_scalar(mixc[:, 1:2], mixc[:, 0:1], -1.0, 1.0, ALU.mult, ALU.add)
                    dve.tensor_scalar(rates[:, 2, :], rates[:, 2, :], -1.0, None, ALU.mult).then_inc(rates_sb, 1)
                if h == 1:
                    route_part(0, 0, 0)
                mix(0)
                mix(1)
                for n in range(BH):
                    if n >= 1:
                        times_v(n - 1)
                    dve.wait_ge(a_kvr, h * BH + n + 1)
                    dve.tensor_scalar(kmin[:, n % 2, :, :], pair(n)[:, :, 0:DIM], K_CLAMP, None, ALU.min
                                      ).then_inc(a_kmin, 1)
                    if h == 1 and n in ROUTE_AT_A:
                        route_part(0, 0, 1 + ROUTE_AT_A.index(n))
                    if n % 2 == 1 and n // 2 + 2 < GROUPS:
                        mix(n // 2 + 2)
                times_v(BH - 1)
                dve.wait_ge(a_gate, h + 1)

                def reciprocal(n):
                    dve.wait_ge(a_den, h * 8 + n + 1)
                    if n >= 3:
                        dve.wait_ge(a_rw, h * 8 + n - 2)
                    dve.reciprocal(rec[:, n % 3], den[:, n % 2]).then_inc(a_rec, 1)
                reciprocal(0)
                for n in range(8):
                    if n + 1 < 8:
                        reciprocal(n + 1)
                    dve.wait_ge(a_rec, h * 8 + n + 1)
                    heads = W(n)[:, :].rearrange("p (i b k c) -> p i b k c", i=4, b=BH, k=2)
                    dve.tensor_tensor(rec[:, n % 3], heads[:, :, :, 1, :], rec[:, n % 3], ALU.mult
                                      ).then_inc(a_ratio, 1)
                add_rows(ch, h, h * GROUPS, a_out, h * GROUPS)
                ch.close()

            def wide(ap):
                return ap.unsqueeze(2).to_broadcast([P, TH, EXPERTS])

            routes = [Chain(dve, dve_r, r * R_STEPS, R_STEPS) for r in range(2 * HALVES)]

            def route_front(m, h):
                dve.wait_ge(xn_free, 2 * m + h + 1)
                layernorm(routes[2 * m + h], h, 1, r_stats, xn_moe, r_normv, mean_square=square[:, 3, 0:TH])

            def route_part(m, h, part):
                r = 2 * m + h
                ch = routes[r]
                tt, ts, stt = dve.tensor_tensor, dve.tensor_scalar, dve.scalar_tensor_tensor
                if part == 0:
                    dve.wait_ge(r_dot, (r + 1) * GROUPS)
                    dot = B(7)[:, 0:TH * EXPERTS].rearrange("p (t e) -> p t e", t=TH)
                    ch.step(stt(dist[:, :, :], dot, -2.0,
                                cent_sq[:, :].unsqueeze(1).to_broadcast([P, TH, EXPERTS]), ALU.mult, ALU.add))
                    ch.step(ts(square[:, 2, 0:TH], square[:, 3, 0:TH], float(DIM), None, ALU.mult))
                    ch.step(tt(dist[:, :, :], dist[:, :, :], wide(square[:, 2, 0:TH]), ALU.add))
                    ch.step(ts(dist[:, :, :], dist[:, :, :], DIST_MIN, None, ALU.max))
                if part in (1, 2):
                    c = part - 1
                    ch.step(dve.tensor_reduce(top[:, c, :], dist[:, :, :], AX.X, ALU.max))
                    ch.step(tt(t8[:, :, :], dist[:, :, :], wide(top[:, c, :]), ALU.is_equal))
                    ch.step(tt(t8[:, :, :], t8[:, :, :], rank[:, :, :], ALU.mult))
                    ch.step(dve.tensor_reduce(far[:, 0, :], t8[:, :, :], AX.X, ALU.max))
                    ch.step(tt(onehot[:, c, :, :], t8[:, :, :], wide(far[:, 0, :]), ALU.is_equal))
                    if c == 0:
                        ch.step(stt(dist[:, :, :], onehot[:, 0, :, :], -3.0e38, dist[:, :, :], ALU.mult, ALU.add))
                if part == 2:
                    tt(mask[:, :, :], onehot[:, 0, :, :], onehot[:, 1, :, :], ALU.add).then_inc(r_mask, 1)
                if part == 3:
                    rsqrt(ch, square[:, 0, 0:2 * TH], top[:, :, :].rearrange("p c t -> p (c t)"), square[:, 1, 0:2 * TH])
                    ch.step(tt(square[:, 0, 0:2 * TH], square[:, 0, 0:2 * TH],
                               top[:, :, :].rearrange("p c t -> p (c t)"), ALU.mult))
                    tt(far[:, 0, :], square[:, 0, TH:2 * TH], square[:, 0, 0:TH], ALU.subtract).then_inc(r_gap, 1)
                if part == 4:
                    dve.wait_ge(r_count, r + 1)
                    ch.step(dve.tensor_copy(counts[:, :, :], B(7)[:, P:P + TH * EXPERTS].rearrange("p (t e) -> p e t", t=TH)))
                    ch.step(dve.tensor_tensor_scan(upto[:, :, :].rearrange("p e t -> p (e t)"),
                                                   not_first[:, :, :].rearrange("p e t -> p (e t)"),
                                                   counts[:, :, :].rearrange("p e t -> p (e t)"), 0.0,
                                                   ALU.mult, ALU.add))
                    ch.step(ts(exp_i[:, :], upto[:, :, TH - 1], float(P - 1), None, ALU.add))
                    ch.step(ts(exp_i[:, :], exp_i[:, :], P.bit_length() - 1, None, ALU.arith_shift_right))
                    ch.step(dve.tensor_copy(exp_e[:, 0, :], exp_i[:, :]))
                    ch.step(dve.tensor_tensor_scan(exp_e[:, 1, :], ones[:, 0:EXPERTS], exp_e[:, 0, :], 0.0,
                                                   ALU.mult, ALU.add))
                    ch.step(tt(exp_e[:, 2, :], exp_e[:, 1, :], exp_e[:, 0, :], ALU.subtract))
                    ch.step(ts(exp_e[:, 2, :], exp_e[:, 2, :], float(P), None, ALU.mult))
                    ch.step(tt(upto[:, :, :], upto[:, :, :], counts[:, :, :], ALU.subtract))
                    ch.step(tt(upto[:, :, :], upto[:, :, :],
                               exp_e[:, 2, :].unsqueeze(2).to_broadcast([P, EXPERTS, TH]), ALU.add))
                    ch.step(tt(dist[:, :, :], upto[:, :, :].rearrange("p e t -> p t e"),
                               B(7)[:, 2 * P:2 * P + TH * EXPERTS].rearrange("p (t e) -> p t e", t=TH), ALU.add))
                    dve.sem_inc(r_read, 1)
                if part == 5:
                    for c in range(2):
                        ch.step(tt(t8[:, :, :], dist[:, :, :], onehot[:, c, :, :], ALU.mult))
                        ch.step(dve.tensor_reduce(pos_f[:, :, c], t8[:, :, :], AX.X, ALU.add))
                    half_slots = slot_of[:, h:h + 1, :, :].rearrange("p a t c -> p (a t c)")
                    ch.step(ts(half_slots, pos_f[:, :, :].rearrange("p t c -> p (t c)"), half_base[:, h:h + 1], None,
                               ALU.add))
                    ch.step(tt(slot_cmp[:, :, :], slot_no[:, :, :],
                               exp_e[:, 1, :].unsqueeze(1).to_broadcast([P, SLOT_TILES, EXPERTS]), ALU.is_ge))
                    ch.step(dve.tensor_reduce(slot_f[:, :], slot_cmp[:, :, :], AX.X, ALU.add))
                    ts(expert_of[:, h * SLOT_TILES:(h + 1) * SLOT_TILES], slot_f[:, :], float(EXPERTS - 1), None,
                       ALU.min).then_inc(r_routed, 1)
                if part == 6:
                    dve.wait_ge(r_exp, r + 1)
                    ch.step(ts(top[:, 0, :], far[:, 1, :], 1.0, None, ALU.add))
                    ch.step(dve.reciprocal(top[:, 1, :], top[:, 0, :]))
                    both = weight[:, h:h + 1, :, :].rearrange("p a t c -> p (a t) c")
                    dve.tensor_copy(both[:, :, 0], top[:, 1, :])
                    ch.step(tt(both[:, :, 1], top[:, 1, :], far[:, 1, :], ALU.mult))
                    ch.close()

            def expert_tile(i, at, expert):
                live = isinstance(at.start, int)
                if not live or 0 <= i < ALL_SLOT_TILES:
                    e = expert(i)
                    dve.wait_ge(e_g, at(i + 1))
                    dve.tensor_tensor(ex_g[:, i % 2, :], B(1 + i % 2)[:, 0:HID], flat(bias_gu[:, bass.ds(e, 1), 0, :]),
                                      ALU.add).then_inc(e_gb, 1)
                    dve.wait_ge(e_u, at(i + 1))
                    dve.tensor_tensor(ex_u[:, i % 2, :], B(3 + i % 2)[:, 0:HID], flat(bias_gu[:, bass.ds(e, 1), 1, :]),
                                      ALU.add).then_inc(e_ub, 1)
                if not live or 0 <= i - 3 < ALL_SLOT_TILES:
                    e = expert(i - 3)
                    if live:
                        wait_from(dve, e_y_out[i % 3], 16 * (at.start // 3 + (i - 3) // 3))
                    else:
                        dve.wait_ge(e_y_out[i % 3], at.third(16 * ((i - 3) // 3)))
                    dve.wait_ge(e_y, at(i - 2))
                    dve.tensor_tensor(ex_y[:, i % 3, :], B(7)[:, 0:P], flat(bias_2[:, bass.ds(e, 1), :]), ALU.add
                                      ).then_inc(e_yb, 1)
                if not live or 0 <= i < ALL_SLOT_TILES:
                    dve.wait_ge(e_ub, at(i + 1))
                    dve.wait_ge(e_silu, at(i + 1))
                    dve.tensor_tensor(ex_h[:, i % 3, :], ex_s[:, i % 2, :], ex_u[:, i % 2, :], ALU.mult
                                      ).then_inc(e_h, 1)

            def combine(ch, m, h, g):
                dve.wait_ge(gathered[g], (2 * m + h + 1) * 16 * 2 * 4)
                for c in range(2):
                    for t in range(4 * g, 4 * g + 4):
                        last = dve.scalar_tensor_tensor(
                            X[:, h * TH + t, :], picked[:, t, c, :], weight[:, h, t, c:c + 1],
                            X[:, h * TH + t, :], ALU.mult, ALU.add)
                    ch.step(last)
                if g == GROUPS - 1:
                    dve.sem_inc(b_x, 1)

            def combined(m, h, g):
                if m == 0:
                    row_stats(h, g).then_inc(b_rows, 1)
                else:
                    dve.sem_inc(f_done, 1)

            first_half = [Chain(dve, dve_b, 0, B_STEPS), Chain(dve, dve_f, 0, F_STEPS)]

            def last_tiles(m):
                def run(i, at, expert):
                    expert_tile(i, at, expert)
                    k = i - (ALL_SLOT_TILES - UNROLL)
                    if isinstance(at.start, int) and 0 <= k < 2 * GROUPS:
                        if k % 2 == 0:
                            combine(first_half[m], m, 0, k // 2)
                        else:
                            combined(m, 0, k // 2)
                return run

            def channel_round(h):
                ch = first_half[0] if h == 0 else Chain(dve, dve_b, h * B_STEPS, B_STEPS)
                tt, ts = dve.tensor_tensor, dve.tensor_scalar
                for g in range(GROUPS if h == 1 else 0):
                    combine(ch, 0, h, g)
                    combined(0, h, g)
                dve.wait_ge(b_rows, (h + 1) * GROUPS)
                layernorm(ch, h, 0, b_stats, xn, b_normv, rms=True)

                def copy_qk(n):
                    dve.wait_ge(b_qk, h * BH + n + 1)
                    if n >= 2:
                        dve.wait_ge(b_gram, h * BH + n - 1)
                    dve.tensor_copy(qk[:, n % 2, :, :], B(2 + n % 2)[:, :].rearrange("p (t c) -> p t c", t=2)
                                    ).then_inc(b_qks, 1)

                def blocks(g):
                    dve.wait_ge(b_gram, h * BH + 2 * g + 2)
                    src = B(4 + g % 2)[:, :].rearrange("p (s k c) -> p s k c", s=2, k=2)
                    for s in range(2):
                        last = tt(gram[:, s, :, :, :].rearrange("p k a c -> p k (a c)"), src[:, s, :, :],
                                  same_head[:, :, :].rearrange("p a c -> p (a c)").unsqueeze(1).to_broadcast(
                                      [P, 2, P]), ALU.mult)
                    ch.step(last)
                    ch.step(dve.tensor_reduce(sims[:, 2 * g:2 * g + 2, :, :].rearrange("p s k c -> p (s k) c"),
                                              gram[:, :, :, :, :].rearrange("p s k a c -> p (s k) c a"), AX.X, ALU.add))
                    dve.sem_inc(b_ext, 1)
                if h == 1:
                    route_part(1, 0, 0)
                for n in range(BH):
                    copy_qk(n)
                    if h == 1 and n in ROUTE_AT_B:
                        route_part(1, 0, 1 + ROUTE_AT_B.index(n))
                    if n % 2 == 0 and n >= 2:
                        blocks(n // 2 - 1)
                blocks(GROUPS - 1)
                ch.step(ts(qnorm[:, :], B(6)[:, 0:BH], 1e-24, None, ALU.max))
                rsqrt(ch, small[:, 2, 0:BH], qnorm[:, :], small[:, 1, 0:BH])
                ch.step(ts(small[:, 2, 0:BH], small[:, 2, 0:BH], mixc[:, 3:4], None, ALU.mult))
                knorm = small[:, 3, :]
                ch.step(ts(knorm.rearrange("p (b c) -> p b c", b=BH), sims[:, :, 1, :], 1e-24, None, ALU.max))
                rsqrt(ch, small[:, 0, :], knorm, small[:, 1, :])
                ch.step(tt(att[:, :, :], sims[:, :, 0, :], small[:, 0, :].rearrange("p (b c) -> p b c", b=BH),
                           ALU.mult))

                def row(ap):
                    return ap.unsqueeze(2).to_broadcast([P, BH, DH_B])
                ch.step(tt(att[:, :, :], att[:, :, :], row(small[:, 2, 0:BH]), ALU.mult))
                ch.step(dve.tensor_reduce(qnorm[:, :], att[:, :, :], AX.X, ALU.max))
                tt(att[:, :, :], att[:, :, :], row(qnorm[:, :]), ALU.subtract).then_inc(b_shift, 1)
                dve.wait_ge(b_exp, h + 1)
                ch.step(dve.tensor_reduce(qnorm[:, :], att[:, :, :], AX.X, ALU.add))
                ch.step(dve.reciprocal(small[:, 2, 0:BH], qnorm[:, :]))
                ch.step(tt(att[:, :, :], att[:, :, :], row(small[:, 2, 0:BH]), ALU.mult))
                for s in range(BH):
                    last = tt(att_diag[:, s, :, :], att[:, s, :].unsqueeze(1).to_broadcast([P, HEADS_B, DH_B]),
                              same_head[:, :, :], ALU.mult)
                    if s % 4 == 3:
                        last.then_inc(b_diag, 1)
                add_rows(ch, h, (HALVES + h) * GROUPS, b_out, h * GROUPS)
                ch.close()

            dve.memset(wgu[:, :, :, :].rearrange("p e n h -> p (e n h)")[:, 0:13 * DIM], 0.0).then_inc(memsets, 1)
            dve.memset(half_base[:, 0:1], 0.0)
            dve.memset(half_base[:, 1:2], float(SLOT_TILES * P))
            dve.sem_inc(b_x, 1)
            for h in range(HALVES):
                rwkv_round(h)
                route_front(0, h)
            for part in range(ROUTE_PARTS):
                route_part(0, 1, part)
            dve.wait_ge(wgu_in, 64)
            dve.wait_ge(w2_in, 32)
            expert_loop(nc, dve, 0, expert_of, last_tiles(0), 0)
            for h in range(HALVES):
                channel_round(h)
                route_front(1, h)
            for part in range(ROUTE_PARTS):
                route_part(1, 1, part)
            expert_loop(nc, dve, 1, expert_of, last_tiles(1), 0)
            first_half[1].close()
            ch = Chain(dve, dve_f, F_STEPS, F_STEPS)
            for g in range(GROUPS):
                combine(ch, 1, 1, g)
                combined(1, 1, g)
            ch.close()

        @block.tensor
        def _(pe):
            def mm(o, l, r, start=True, stop=True):
                return pe.matmul(o, l, r, start=start, stop=stop)

            pe.wait_ge(consts, 3)
            pe.wait_ge(raw_in, 16 * 7)
            for n in range(4):
                pe.transpose(B(6)[:, n * P:(n + 1) * P], raw[:, n, :], ident[:, :])
            for n, w in enumerate((4, 5, 7)):
                pe.transpose(B(7)[:, n * P:(n + 1) * P], raw[:, w, :], ident[:, :])
            pe.transpose(B(7)[:, 3 * P:3 * P + EXPERTS], cent[:, :], ident[0:EXPERTS, 0:EXPERTS]
                         ).then_inc(setup_ps, 1)
            pe.wait_ge(setup_sb, 2)
            mm(B(7)[:, 4 * P - EXPERTS:4 * P], ones[:, :], centT2[:, :]).then_inc(setup_ps, 1)

            def rwkv_round(h):
                def transposes(g):
                    if g < 2:
                        pe.wait_ge(a_normv, 2 * h + g + 1)
                    else:
                        pe.wait_ge(a_norm, 2 * h + g - 1)
                    if g >= 2:
                        pe.wait_ge(a_mixed, h * GROUPS + g - 1)
                    for t in range(4):
                        last = pe.transpose(B(g % 2)[:, t * P:(t + 1) * P], xn[:, 4 * g + t, :], ident[:, :])
                    last.then_inc(a_xT, 1)
                transposes(0)
                transposes(1)
                for n in range(BH):
                    if n % 2 == 0:
                        pe.wait_ge(a_mixed, h * GROUPS + n // 2 + 1)
                    if n >= 2:
                        pe.wait_ge(a_kv, h * BH + n - 1)
                    for t in range(2):
                        c = 2 * (n % 2) + t
                        last = mm(pair(n)[:, t, 0:3 * DIM], mixed[:, n // 2 % 2, c * P:(c + 1) * P],
                                  wT[:, :, :].rearrange("p n c -> p (n c)"))
                    last.then_inc(a_kvr, 1)
                    if h == 1 and n == COUNT_AT_A:
                        count(0, 0)
                    if n % 2 == 1 and n // 2 + 2 < GROUPS:
                        transposes(n // 2 + 2)
                pe.wait_ge(a_kv, (h + 1) * BH)
                pe.wait_ge(masked, 2)
                for n in range(8):
                    i, par = n // 2, n % 2
                    if h == 1 and n == 5:
                        pe.wait_ge(r_read, 1)
                    if n >= 6:
                        pe.wait_ge(a_ratio, h * 8 + n - 5)
                    for hd in range(4 * i, 4 * i + 4):
                        o = W(n)[:, (hd - 4 * i) * P:(hd - 4 * i + 1) * P]
                        cols = slice(DH_A * hd, DH_A * hd + DH_A)
                        if par == 0:
                            last = mm(o, decay[:, hd, 0:P], kv[:, 0:TH:2, :, cols])
                        else:
                            mm(o, decay[:, hd, P:2 * P], kv[:, 0:TH:2, :, cols], stop=False)
                            last = mm(o, decay[:, hd, 0:P], kv[:, 1:TH:2, :, cols], start=False)
                    last.then_inc(a_wkv, 1)
                pe.wait_ge(a_rw, (h + 1) * 8)

                def back(g):
                    if g >= 2:
                        pe.wait_ge(a_rTs, h * GROUPS + g - 1)
                    for t in range(4):
                        last = pe.transpose(B(g % 2)[:, t * P:(t + 1) * P], rwkv[:, 4 * g + t, :], ident[:, :])
                    last.then_inc(a_rT, 1)
                back(0)
                for g in range(GROUPS):
                    if g + 1 < GROUPS:
                        back(g + 1)
                    pe.wait_ge(a_rTs, h * GROUPS + g + 1)
                    if g >= 2:
                        pe.wait_ge(a_x, h * GROUPS + g - 1)
                    for t in range(4):
                        last = mm(B(6 + g % 2)[:, t * P:(t + 1) * P], yT[:, g % 2, t * P:(t + 1) * P], woT[:, :])
                    last.then_inc(a_out, 1)

            def route_round(m, h):
                r = 2 * m + h

                def transposes(g):
                    if g < 2:
                        pe.wait_ge(r_normv, 2 * r + g + 1)
                    else:
                        pe.wait_ge(r_norm, 2 * r + g - 1)
                    if g >= 2:
                        pe.wait_ge(r_xTs, r * GROUPS + g - 1)
                    for t in range(4):
                        last = pe.transpose(B(g % 2)[:, t * P:(t + 1) * P], xn_moe[:, 4 * g + t, :], ident[:, :])
                    last.then_inc(r_xT, 1)
                transposes(0)
                for g in range(GROUPS):
                    if g + 1 < GROUPS:
                        transposes(g + 1)
                    pe.wait_ge(r_xTs, r * GROUPS + g + 1)
                    for t in range(4):
                        c = (4 * g + t) * EXPERTS
                        last = mm(B(7)[:, c:c + EXPERTS], yT[:, g % 2, t * P:(t + 1) * P], centT[:, :])
                    last.then_inc(r_dot, 1)

            def count(m, h):
                pe.wait_ge(r_mask, 2 * m + h + 1)
                chosen = mask[:, :, :].rearrange("p t e -> p (t e)")
                mm(B(7)[:, P:P + TH * EXPERTS], ones[:, :], chosen)
                mm(B(7)[:, 2 * P:2 * P + TH * EXPERTS], later[:, :], chosen).then_inc(r_count, 1)

            def expert_tile(i, at, expert):
                live = isinstance(at.start, int)
                if not live or 0 <= i < ALL_SLOT_TILES:
                    e = expert(i)
                    pe.wait_ge(e_xTs, at(i + 1))
                    mm(B(1 + i % 2)[:, 0:HID], ex_xT[:, i % 2, :], flat(wgu[:, bass.ds(e, 1), 0, :])).then_inc(e_g, 1)
                    wait_from(pe, e_ub, at(i - 1))
                    mm(B(3 + i % 2)[:, 0:HID], ex_xT[:, i % 2, :], flat(wgu[:, bass.ds(e, 1), 1, :])).then_inc(e_u, 1)
                if not live or i + 1 < ALL_SLOT_TILES:
                    n = i + 1
                    if live:
                        pe.wait_ge(e_x_in[n % UNROLL], 16 * (at.start // UNROLL + n // UNROLL + 1))
                    else:
                        pe.wait_ge(e_x_in[n % UNROLL], at.round(16 * (n // UNROLL + 1)))
                    pe.transpose(B(0)[:, 0:P], ex_x[:, n % UNROLL, :], ident[:, :]).then_inc(e_xT, 1)
                if not live or 0 <= i - 2 < ALL_SLOT_TILES:
                    pe.wait_ge(e_h, at(i - 1))
                    for c in range(NCH):
                        if c == 1:
                            wait_from(pe, e_yb, at(i - 3))
                        last = pe.transpose(B(5 + i % 2)[0:CH, c * P:(c + 1) * P],
                                            ex_h[:, (i - 2) % 3, c * CH:(c + 1) * CH], ident[:, :])
                    last.then_inc(e_hT, 1)
                if not live or 0 <= i - 3 < ALL_SLOT_TILES:
                    e = expert(i - 3)
                    if live and i - 2 >= ALL_SLOT_TILES:
                        wait_from(pe, e_yb, at(i - 3))
                    pe.wait_ge(e_hTs, at(i - 2))
                    for c in range(NCH):
                        last = mm(B(7)[:, 0:P], ex_hT[:, (i - 3) % 2, c, :], flat(w2[:, bass.ds(e, 1), c, :]),
                                  start=(c == 0), stop=(c == NCH - 1))
                    last.then_inc(e_y, 1)

            def channel_round(h):
                def transposes(g):
                    if g < 2:
                        pe.wait_ge(b_normv, 2 * h + g + 1)
                    else:
                        pe.wait_ge(b_norm, 2 * h + g - 1)
                    if g >= 2:
                        pe.wait_ge(b_xTs, h * GROUPS + g - 1)
                    for t in range(4):
                        last = pe.transpose(B(g % 2)[:, t * P:(t + 1) * P], xn[:, 4 * g + t, :], ident[:, :])
                    last.then_inc(b_xT, 1)

                def qk_of(n):
                    pe.wait_ge(b_xTs, h * GROUPS + n // 2 + 1)
                    if n >= 2:
                        pe.wait_ge(b_qks, h * BH + n - 1)
                    for t in range(2):
                        last = mm(B(2 + n % 2)[:, t * 2 * P:(t + 1) * 2 * P], xT_half[:, 2 * n + t, :],
                                  wqkT[:, :, :].rearrange("p n c -> p (n c)"))
                    last.then_inc(b_qk, 1)

                def gram_of(n):
                    s, g = n % 2, n // 2
                    pe.wait_ge(b_sq, h * BH + n + 1)
                    if g >= 2 and s == 0:
                        pe.wait_ge(b_ext, h * GROUPS + g - 1)
                    o = B(4 + g % 2)[:, s * 2 * P:(s + 1) * 2 * P]
                    for t in range(2):
                        mm(o[:, 0:P], qk[:, s, t, 0:P], qk[:, s, t, P:2 * P], start=(t == 0), stop=(t == 1))
                    for t in range(2):
                        mm(o[:, P:2 * P], ones[:, :], qk_sq[:, s, t, P:2 * P], start=(t == 0), stop=(t == 1))
                    for t in range(2):
                        last = mm(B(6)[:, n:n + 1], qk_sq[:, s, t, 0:P], ones[:, 0:1], start=(t == 0), stop=(t == 1))
                    last.then_inc(b_gram, 1)
                transposes(0)
                qk_of(0)
                for g in range(GROUPS):
                    if g + 1 < GROUPS:
                        transposes(g + 1)
                    qk_of(2 * g + 1)
                    gram_of(2 * g)
                    if g + 1 < GROUPS:
                        qk_of(2 * g + 2)
                    gram_of(2 * g + 1)
                    if h == 1 and g == 1:
                        count(1, 0)
                for q in range(2):
                    pe.wait_ge(b_diag, 2 * h + q + 1)
                    if q == 1:
                        pe.wait_ge(b_ms, 2 * h + q)
                    for s in range(4):
                        last = mm(B(4)[:, s * P:(s + 1) * P],
                                  att_diag[:, 4 * q + s, :, :].rearrange("p a c -> p (a c)"), w_outT[:, :])
                    last.then_inc(b_m, 1)
                    pe.wait_ge(b_ms, 2 * h + q + 1)
                    mm(B(5)[:, :], raw[:, 6, :], folded[:, 0, :, :].rearrange("p b c -> p (b c)")).then_inc(b_p, 1)
                    pe.wait_ge(b_pss, 2 * h + q + 1)
                    for g in range(2 * q, 2 * q + 2):
                        if g >= 2:
                            pe.wait_ge(a_x, h * GROUPS + GROUPS * HALVES + g - 1)
                        for t in range(4):
                            last = mm(B(6 + g % 2)[:, t * P:(t + 1) * P], xT_half[:, 4 * g + t, :],
                                      folded[:, 1, 2 * (g % 2) + t // 2, :])
                        last.then_inc(b_out, 1)

            for h in range(HALVES):
                rwkv_round(h)
                route_round(0, h)
            count(0, 1)
            pe.wait_ge(wgu_in, 64)
            pe.wait_ge(w2_in, 32)
            pe.wait_ge(r_read, HALVES)
            expert_loop(nc, pe, 0, expert_of, expert_tile, -1)
            for h in range(HALVES):
                channel_round(h)
                route_round(1, h)
            count(1, 1)
            pe.wait_ge(r_read, 2 * HALVES)
            expert_loop(nc, pe, 1, expert_of, expert_tile, -1)


_INS = ["L0_attn_a_x", "L0_attn_a_time_decay", "L0_attn_a_time_first", "L0_attn_a_time_mix", "L0_attn_a_Wk",
        "L0_attn_a_Wv", "L0_attn_a_Wr", "L0_attn_a_Wo", "L0_attn_b_norm_weight", "L0_attn_b_w_qkv",
        "L0_attn_b_temperature", "L0_attn_b_w_out", "L0_ffn_centroid", "L0_ffn_Wg", "L0_ffn_bg", "L0_ffn_W1",
        "L0_ffn_b1", "L0_ffn_W2", "L0_ffn_b2"]


def kernel(**inputs):
    import numpy as np
    import concourse.bacc as bacc
    from concourse.bass_utils import run_bass_kernel_spmd as run

    nc = bacc.Bacc("TRN2", target_bir_lowering=False, num_devices=1)
    arrays, aps = {}, {}
    for name in _INS:
        a = np.ascontiguousarray(inputs[name])
        arrays[f"in_{name}"] = a
        aps[name] = nc.dram_tensor(f"in_{name}", a.shape, mybir.dt.from_np(a.dtype), kind="ExternalInput").ap()
    out = nc.dram_tensor("out_0", (BATCH, SEQ, DIM), mybir.dt.float32, kind="ExternalOutput").ap()
    build(nc, aps, out)
    return run(nc, [arrays], core_ids=[0]).results[0]["out_0"]
```
